# Optimizing a Trainium2 kernel written in Bass

```python
import numpy as np
import jax
import jax.numpy as jnp

def _softmax(x, axis=-1):
    return jax.nn.softmax(x, axis=axis)

def _gelu(x):
    return jax.nn.gelu(x, approximate=True)

def _silu(x):
    return jax.nn.silu(x)

def _sigmoid(x):
    return jax.nn.sigmoid(x)

def _layernorm(x, axis=-1, eps=1e-05):
    m = jnp.mean(x, axis=axis, keepdims=True)
    v = jnp.var(x, axis=axis, keepdims=True)
    return (x - m) / jnp.sqrt(v + eps)

def _scatter_add(tgt, idx, src, axis=0):
    return tgt.at[idx].add(src)

def _segment_sum(src, seg, n):
    return jax.ops.segment_sum(src, seg, n)
kernel_name = 'mk_macaron_d1_jaxref_r8_3186ab'

def setup_inputs(seed: int=0):
    np.random.seed(seed)
    _w = jnp.asarray

    def _L0_attn_setup():
        import jax, jax.numpy as jnp
        import numpy as np
        from jax import lax
        B, L, D = (4, 256, 256)
        R = 256
        DH = D // 4
        key = jax.random.key(seed)
        ks = jax.random.split(key, 12)
        s = 0.02
        x = jax.random.normal(ks[0], (B, L, D), dtype=jnp.float32)
        Wu = jax.random.normal(ks[1], (R, D), dtype=jnp.float32) * s
        bu = jnp.zeros((R,), dtype=jnp.float32)
        Wv = jax.random.normal(ks[2], (R, D), dtype=jnp.float32) * s
        bv = jnp.zeros((R,), dtype=jnp.float32)
        Wg1 = jax.random.normal(ks[3], (DH, D), dtype=jnp.float32) * s
        bg1 = jnp.zeros((DH,), dtype=jnp.float32)
        Wg2 = jax.random.normal(ks[4], (R, DH), dtype=jnp.float32) * s
        bg2 = jnp.zeros((R,), dtype=jnp.float32)
        conv_w = jax.random.normal(ks[5], (D, 1, 3), dtype=jnp.float32) * s
        conv_b = jnp.zeros((D,), dtype=jnp.float32)
        return {'x': x, 'Wu': Wu, 'bu': bu, 'Wv': Wv, 'bv': bv, 'Wg1': Wg1, 'bg1': bg1, 'Wg2': Wg2, 'bg2': bg2, 'conv_w': conv_w, 'conv_b': conv_b}
    _L0_attn_in = _L0_attn_setup()

    def _L0_ffn_setup():
        import jax, jax.numpy as jnp
        import numpy as np
        E = 64
        K = 6
        NG = 8
        TKG = 4
        SCALE = 2.5
        CAP = 64

        def _router(x, gate_w, e_bias):
            logits = x.astype(jnp.float32) @ gate_w.T
            scores = jax.nn.sigmoid(logits)
            sc = scores + e_bias[None, :]
            T = x.shape[0]
            gs = sc.reshape(T, NG, E // NG)
            grp_score = jax.lax.top_k(gs, 2)[0].sum(-1)
            _, gidx = jax.lax.top_k(grp_score, TKG)
            gmask = jax.nn.one_hot(gidx, NG, dtype=sc.dtype).sum(1)
            emask = jnp.repeat(gmask, E // NG, axis=1)
            masked = jnp.where(emask > 0, sc, -jnp.inf)
            _, idx = jax.lax.top_k(masked, K)
            w = jnp.take_along_axis(scores, idx, axis=1)
            w = w / (w.sum(-1, keepdims=True) + 1e-20) * SCALE
            return (idx, w)

        def _relu2(h):
            return jnp.square(jax.nn.relu(h))

        def _moe(x, idx, w, w1, w2):
            T, D = x.shape
            e_flat = idx.reshape(-1)
            tok = jnp.repeat(jnp.arange(T), K)
            oh = jax.nn.one_hot(e_flat, E, dtype=jnp.float32)
            pos = jnp.cumsum(oh, axis=0) - oh
            pos = (pos * oh).sum(-1).astype(jnp.int32)
            keep = pos < CAP
            slot = jnp.where(keep, pos, CAP)
            xd = jnp.zeros((E, CAP + 1, D), x.dtype).at[e_flat, slot].set(x[tok])
            h = _relu2(jnp.einsum('ecd,eid->eci', xd, w1))
            yd = jnp.einsum('eci,edi->ecd', h, w2)
            gate = w.reshape(-1)[:, None] * keep[:, None].astype(x.dtype)
            y_assign = yd[e_flat, slot] * gate
            return jnp.zeros((T, D), x.dtype).at[tok].add(y_assign)
        key = jax.random.key(seed)
        ks = jax.random.split(key, 6)
        D, I, SH, T = (256, 128, 512, 256)
        x = jax.random.normal(ks[0], (1, T, D), jnp.float32)
        gate_w = jax.random.normal(ks[1], (E, D), jnp.float32) * D ** (-0.5)
        e_bias = jnp.zeros((E,), jnp.float32)
        w1 = jax.random.normal(ks[2], (E, I, D), jnp.float32) * D ** (-0.5)
        w2 = jax.random.normal(ks[3], (E, D, I), jnp.float32) * I ** (-0.5)
        su = jax.random.normal(ks[4], (SH, D), jnp.float32) * D ** (-0.5)
        sd = jax.random.normal(ks[5], (D, SH), jnp.float32) * SH ** (-0.5)
        return {'hidden_states': x, 'gate_w': gate_w, 'e_bias': e_bias, 'w1': w1, 'w2': w2, 'shared_up_w': su, 'shared_down_w': sd}
    _L0_ffn_in = _L0_ffn_setup()
    _d = {'L0_attn_x': _L0_attn_in['x'], 'L0_attn_Wu': _L0_attn_in['Wu'], 'L0_attn_bu': _L0_attn_in['bu'], 'L0_attn_Wv': _L0_attn_in['Wv'], 'L0_attn_bv': _L0_attn_in['bv'], 'L0_attn_Wg1': _L0_attn_in['Wg1'], 'L0_attn_bg1': _L0_attn_in['bg1'], 'L0_attn_Wg2': _L0_attn_in['Wg2'], 'L0_attn_bg2': _L0_attn_in['bg2'], 'L0_attn_conv_w': _L0_attn_in['conv_w'], 'L0_attn_conv_b': _L0_attn_in['conv_b'], 'L0_ffn_gate_w': _L0_ffn_in['gate_w'], 'L0_ffn_e_bias': _L0_ffn_in['e_bias'], 'L0_ffn_w1': _L0_ffn_in['w1'], 'L0_ffn_w2': _L0_ffn_in['w2'], 'L0_ffn_shared_up_w': _L0_ffn_in['shared_up_w'], 'L0_ffn_shared_down_w': _L0_ffn_in['shared_down_w']}
    _x0 = _d['L0_attn_x']
    _d['L0_attn_x'] = jax.random.normal(jax.random.fold_in(jax.random.key(seed), 1), (8, 256, 256), dtype=_x0.dtype)
    del _x0
    return _d

def reference(L0_attn_x, L0_attn_Wu, L0_attn_bu, L0_attn_Wv, L0_attn_bv, L0_attn_Wg1, L0_attn_bg1, L0_attn_Wg2, L0_attn_bg2, L0_attn_conv_w, L0_attn_conv_b, L0_ffn_gate_w, L0_ffn_e_bias, L0_ffn_w1, L0_ffn_w2, L0_ffn_shared_up_w, L0_ffn_shared_down_w):

    def _L0_attn_ref(x, Wu, bu, Wv, bv, Wg1, bg1, Wg2, bg2, conv_w, conv_b):
        import jax, jax.numpy as jnp
        import numpy as np
        from jax import lax
        B, L, D = (4, 256, 256)
        R = 256
        DH = D // 4
        xc = jnp.transpose(x, (0, 2, 1))
        t = lax.conv_general_dilated(xc, conv_w, window_strides=(1,), padding=[(1, 1)], dimension_numbers=('NCH', 'OIH', 'NCH'), feature_group_count=D)
        t_out = jnp.transpose(t + conv_b[None, :, None], (0, 2, 1))
        u = jnp.einsum('bld,rd->blr', x, Wu) + bu
        v = jnp.einsum('bld,rd->blr', x, Wv) + bv
        h = jax.nn.relu(jnp.einsum('bld,hd->blh', x, Wg1) + bg1)
        gates = jax.nn.sigmoid(jnp.einsum('blh,rh->blr', h, Wg2) + bg2)
        u_gated = u * gates
        v_gated = v * gates
        k_cumsum = jnp.cumsum(u_gated, axis=1)
        global_out = k_cumsum * v_gated
        uv_term = jnp.einsum('blr,rd->bld', global_out, Wu.T[:R, :])
        return t_out + uv_term

    def _L0_ffn_ref(hidden_states, gate_w, e_bias, w1, w2, shared_up_w, shared_down_w):
        import jax, jax.numpy as jnp
        import numpy as np
        E = 64
        K = 6
        NG = 8
        TKG = 4
        SCALE = 2.5
        CAP = 64

        def _router(x, gate_w, e_bias):
            logits = x.astype(jnp.float32) @ gate_w.T
            scores = jax.nn.sigmoid(logits)
            sc = scores + e_bias[None, :]
            T = x.shape[0]
            gs = sc.reshape(T, NG, E // NG)
            grp_score = jax.lax.top_k(gs, 2)[0].sum(-1)
            _, gidx = jax.lax.top_k(grp_score, TKG)
            gmask = jax.nn.one_hot(gidx, NG, dtype=sc.dtype).sum(1)
            emask = jnp.repeat(gmask, E // NG, axis=1)
            masked = jnp.where(emask > 0, sc, -jnp.inf)
            _, idx = jax.lax.top_k(masked, K)
            w = jnp.take_along_axis(scores, idx, axis=1)
            w = w / (w.sum(-1, keepdims=True) + 1e-20) * SCALE
            return (idx, w)

        def _relu2(h):
            return jnp.square(jax.nn.relu(h))

        def _moe(x, idx, w, w1, w2):
            T, D = x.shape
            e_flat = idx.reshape(-1)
            tok = jnp.repeat(jnp.arange(T), K)
            oh = jax.nn.one_hot(e_flat, E, dtype=jnp.float32)
            pos = jnp.cumsum(oh, axis=0) - oh
            pos = (pos * oh).sum(-1).astype(jnp.int32)
            keep = pos < CAP
            slot = jnp.where(keep, pos, CAP)
            xd = jnp.zeros((E, CAP + 1, D), x.dtype).at[e_flat, slot].set(x[tok])
            h = _relu2(jnp.einsum('ecd,eid->eci', xd, w1))
            yd = jnp.einsum('eci,edi->ecd', h, w2)
            gate = w.reshape(-1)[:, None] * keep[:, None].astype(x.dtype)
            y_assign = yd[e_flat, slot] * gate
            return jnp.zeros((T, D), x.dtype).at[tok].add(y_assign)
        orig = hidden_states.shape
        x = hidden_states.reshape(-1, orig[-1])
        idx, wts = _router(x, gate_w, e_bias)
        shared = _relu2(x @ shared_up_w.T) @ shared_down_w.T
        routed = _moe(x, idx, wts.astype(x.dtype), w1, w2)
        return (shared + routed).reshape(orig)
    x = L0_attn_x
    x = x + 0.5 * _L0_ffn_ref(_layernorm(x, axis=-1), L0_ffn_gate_w, L0_ffn_e_bias, L0_ffn_w1, L0_ffn_w2, L0_ffn_shared_up_w, L0_ffn_shared_down_w)
    x = x + _L0_attn_ref(_layernorm(x, axis=-1), L0_attn_Wu, L0_attn_bu, L0_attn_Wv, L0_attn_bv, L0_attn_Wg1, L0_attn_bg1, L0_attn_Wg2, L0_attn_bg2, L0_attn_conv_w, L0_attn_conv_b)
    x = x + 0.5 * _L0_ffn_ref(_layernorm(x, axis=-1), L0_ffn_gate_w, L0_ffn_e_bias, L0_ffn_w1, L0_ffn_w2, L0_ffn_shared_up_w, L0_ffn_shared_down_w)
    return x

_drawn_inputs = setup_inputs


def setup_inputs(seed=0):
    import zlib

    import numpy as np

    out = dict(_drawn_inputs(seed))
    spreads = {'L0_attn_bu': (0.0, 0.1),
     'L0_attn_bv': (0.0, 0.1),
     'L0_attn_bg1': (0.0, 0.552),
     'L0_attn_bg2': (0.0, 0.1),
     'L0_attn_conv_b': (0.0, 0.1),
     'L0_ffn_e_bias': (0.0, 0.1)}
    factors = {'L0_attn_Wg1': 3.121}
    for name, (base, spread) in spreads.items():
        noise = np.random.default_rng([zlib.crc32(name.encode()), seed]).standard_normal(out[name].shape)
        drawn = base * np.exp(spread * noise) if base else spread * noise
        out[name] = jnp.asarray(drawn.astype(out[name].dtype))
    for name, factor in factors.items():
        out[name] = (out[name] * factor).astype(out[name].dtype)
    return out
```

```python
from contextlib import ExitStack

import concourse.bass as bass
from concourse import mybir

ALU = mybir.AluOpType
ACT = mybir.ActivationFunctionType
AX = mybir.AxisListType
F32 = mybir.dt.float32
BF16 = mybir.dt.bfloat16
U32 = mybir.dt.uint32

P = 128
EPS = 1e-5
TOPK = 6
NGRP = 8
TOPG = 4
CAP = 64
ROUTE_SCALE = 2.5
HALF = 0.5
FAR = 1e30


def build(nc, x, wexp, gate, ebias, sup, sdown, wu, wv, wg1, wg2, vecs, consts, out):
    T, D = x.shape
    NT = T // P
    KD = D // P
    E = wexp.shape[1]
    I = P
    SH = sup.shape[2]
    HB = SH // P
    GS = E // NGRP
    NP = E // 2
    assert 2 * CAP == P
    CH = 512
    NC = T // CH
    TC = CH // P
    L = 256
    SEQ = CH // L
    DH = wg1.shape[2]
    HT = T // 2
    CHAINS = 2
    EW = 4
    WR = 4
    XGW = D + E
    NLN = 3

    with ExitStack() as ctx:
        def sb(name, shape, dt=F32):
            return ctx.enter_context(nc.sbuf_tensor(name, shape, dt))

        def sem(name):
            return ctx.enter_context(nc.semaphore(name))

        X = sb("X", [P, NT, D])
        XN = sb("XN", [P, NT, D])
        XT = sb("XT", [P, KD, T])
        S = sb("S", [P, NT, D])
        HID = sb("HID", [P, 2, HB, CH])
        W = sb("W", [P, WR, EW, KD * I + D])
        XG = sb("XG", [P, 8, XGW])
        XD = sb("XD", [P, 3, KD, P])
        RH = sb("RH", [P, 3, P])
        HT2 = sb("HT2", [P, 3, P])
        YO = sb("YO", [P, 4, D])
        GC = sb("GC", [P, 4])
        GJ = sb("GJ", [P, 4, 2])
        SCR = sb("SCR", [P, 12288])
        su = sb("su", [P, KD, SH])
        sd = sb("sd", [P, HB, D])
        gw = sb("gw", [P, KD, E])
        eb = sb("eb", [P, E])
        wus = sb("wus", [P, KD, D])
        wvs = sb("wvs", [P, KD, D])
        wg1s = sb("wg1s", [P, KD, DH])
        wg2s = sb("wg2s", [DH, D])
        vec = sb("vec", [P, vecs.shape[1]])
        cst = sb("cst", [P, consts.shape[1]])
        st = sb("st", [P, NT, 6])
        mv = sb("mv", [P, NT, 2])
        rstd = sb("rstd", [P, NT])
        mh = sb("mh", [P, TC])
        maskb = sb("maskb", [P, NT // 2, 2, E], BF16)
        identb = sb("identb", [P, P], BF16)
        gidx = sb("gidx", [P, NP], U32)
        sidx = sb("sidx", [P, NP], U32)
        zero = sb("zero", [P, 512])

        o = 0
        def cut(n):
            nonlocal o
            o += n
            return cst[:, o - n:o]
        ident = cut(P)
        lower = cut(NGRP * NGRP)
        ones = cut(L)
        parity = cut(2)
        half = cut(1)
        slotno = cut(1)
        sel = cut(2 * NP)
        keyrow = cut(HT)
        bu, bv, bg2, cb, cw0, cw1, cw2 = (vec[:, KD * i:KD * (i + 1)] for i in range(7))
        bg1 = vec[0:DH, 7 * KD:7 * KD + 1]

        at = 0
        def take(n):
            nonlocal at
            at += n
            return SCR[:, at - n:at]
        sco = take(NT * E).rearrange("p (t e) -> p t e", e=E)
        scb = take(NT * E).rearrange("p (t e) -> p t e", e=E)
        msk = take(NT * (E + 2)).rearrange("p (t e) -> p t e", e=E + 2)
        rep = take(NT * (E + 2)).rearrange("p (t e) -> p t e", e=E + 2)
        tA = take(NT * E)
        tB = take(NT * E)
        tC = take(NT * E)
        keyA = take(HT)
        keyB = take(HT)
        top = take(NT * 8).rearrange("p (t k) -> p t k", k=8)
        gsc = take(NT * NGRP).rearrange("p (t g) -> p t g", g=NGRP)
        gpen = take(NT * NGRP).rearrange("p (t g) -> p t g", g=NGRP)
        wsum = take(NT)
        wrec = take(NT)
        lst = take(P)
        lstA = take(P)
        lstB = take(P)
        assert at <= 12288
        PL = SCR[:, 0:2 * TC * CHAINS * 2 * D].rearrange("p (b t c d) -> p b t c d", b=2, t=TC, d=D)
        at = 0
        hA = take(CH)
        gT = take(KD * CH).rearrange("p (k t) -> p k t", k=KD)
        ug = take(KD * CH).rearrange("p (k t) -> p k t", k=KD)
        vg = take(KD * CH).rearrange("p (k t) -> p k t", k=KD)
        cum = take(KD * CH).rearrange("p (k t) -> p k t", k=KD)
        go = take(2 * KD * CH).rearrange("p (b k t) -> p b k t", b=2, k=KD)
        cv = take(2 * KD * CH).rearrange("p (b k t) -> p b k t", b=2, k=KD)

        psT = [ctx.enter_context(nc.psum_tensor(f"psT{b}", [P, 512], F32)) for b in range(2)]
        psA = [ctx.enter_context(nc.psum_tensor(f"psA{b}", [P, 512], F32)) for b in range(2)]
        psC = [ctx.enter_context(nc.psum_tensor(f"psC{b}", [P, 512], F32)) for b in range(2)]
        psR = [ctx.enter_context(nc.psum_tensor(f"psR{b}", [P, 512], F32)) for b in range(2)]

        YR = 2 * T + 2 * P
        table = nc.dram_tensor("table", [T, XGW], F32)
        planes = [nc.dram_tensor(f"plane{c}", [YR, D], F32) for c in range(CHAINS)]

        x_loaded = [sem(f"x_loaded{g}") for g in range(NC)]
        const_loaded = sem("const_loaded")
        w_loaded = [sem(f"w_loaded{b}") for b in range(WR)]
        T_full = [sem(f"T_full{b}") for b in range(2)]
        T_free = [sem(f"T_free{b}") for b in range(2)]
        A_full = [sem(f"A_full{b}") for b in range(2)]
        A_free = [sem(f"A_free{b}") for b in range(2)]
        C_full = [sem(f"C_full{b}") for b in range(2)]
        C_free = [sem(f"C_free{b}") for b in range(2)]
        dve_step = sem("dve_step")
        act_step = sem("act_step")
        mean_var = sem("mean_var")
        rstd_ready = sem("rstd_ready")
        xn_ready = sem("xn_ready")
        xt_ready = sem("xt_ready")
        xn_stored = sem("xn_stored")
        gates_ready = sem("gates_ready")
        gates_stored = sem("gates_stored")
        logits_ready = sem("logits_ready")
        scores_ready = sem("scores_ready")
        mask_ready = sem("mask_ready")
        maskT_ready = sem("maskT_ready")
        list_split = sem("list_split")
        list_joined = sem("list_joined")
        slots_ready = sem("slots_ready")
        keyslot_ready = sem("keyslot_ready")
        idx_ready = sem("idx_ready")
        hid_ready = sem("hid_ready")
        shared_ready = sem("shared_ready")
        planes_zero = [sem(f"planes_zero{c}") for c in range(CHAINS)]
        const_made = sem("const_made")
        gathered = [sem(f"gathered{b}") for b in range(8)]
        xd_ready = sem("xd_ready")
        gc_ready = sem("gc_ready")
        relu_ready = sem("relu_ready")
        h_ready = sem("h_ready")
        yo_ready = sem("yo_ready")
        mm1_done = sem("mm1_done")
        mm2_done = sem("mm2_done")
        scattered = [sem(f"scattered{c}") for c in range(CHAINS)]
        plane_loaded = [sem(f"plane_loaded{b}") for b in range(2)]
        plane_used = sem("plane_used")
        hA_ready = sem("hA_ready")
        gT_ready = sem("gT_ready")
        uv_used = sem("uv_used")
        cv_first = sem("cv_first")
        go_ready = sem("go_ready")
        cv_ready = sem("cv_ready")
        att_out = sem("att_out")
        x_final = sem("x_final")
        out_stored = sem("out_stored")

        NPAIR = NT // 2
        T_ln = [0, NPAIR + NP, 2 * NPAIR + NP]
        T_ex = [NPAIR, 3 * NPAIR + NP]
        UP = NC * HB
        NA = 3 + 2 * KD * 2 - 2 + 0
        ATT_A = 1 + 3 * KD
        A_up = [0, UP + NP + NC * ATT_A]
        A_ex = [UP, 2 * UP + NP + NC * ATT_A]
        A_att = UP + NP
        C_dn = [0, NPAIR + NP + NPAIR]
        C_ex = [NPAIR, 3 * NPAIR + NP]
        C_att = NPAIR + NP

        def full(sems, n):
            return sems[n % 2], n // 2 + 1

        NCONST = 12

        x_t = x.rearrange("(t p) d -> p t d", p=P)
        out_t = out.rearrange("(t p) d -> p t d", p=P)
        table_t = table[:, :].rearrange("(t p) w -> p t w", p=P)
        plane_t = [pl[0:2 * T, :].rearrange("(t p c) d -> p t (c d)", p=P, c=2) for pl in planes]

        block = ctx.enter_context(nc.Block())

        @block.sync
        def _(sp):
            loads = [(cst[:, :], consts), (vec[:, :], vecs), (gw[:, :, :], gate), (eb[:, :], ebias),
                     (su[:, :, :], sup), (sd[:, :, :], sdown), (wus[:, :, :], wu), (wvs[:, :, :], wv),
                     (wg1s[:, :, :], wg1), (wg2s[:, :], wg2)]
            sp.dma_start(X[:, 0:TC, :], x_t[:, 0:TC, :]).then_inc(x_loaded[0], 16)
            for dst, src in loads[:4]:
                sp.dma_start(dst, src).then_inc(const_loaded, 16)
            for g in range(1, NC):
                sp.dma_start(X[:, g * TC:(g + 1) * TC, :], x_t[:, g * TC:(g + 1) * TC, :]).then_inc(x_loaded[g], 16)
            for dst, src in loads[4:]:
                sp.dma_start(dst, src).then_inc(const_loaded, 16)

            def load_weights(f, q):
                n = f * (E // EW) + q
                if n >= WR:
                    sp.wait_ge(mm2_done, (n - WR + 1) * (EW // 2))
                sp.dma_start(W[:, n % WR, :, :], wexp[:, q * EW:(q + 1) * EW, :]).then_inc(w_loaded[n % WR], 16)

            for f in range(2):
                for g in range(NC):
                    sp.wait_ge(xn_ready, (2 * f * NC) + g + 1)
                    sp.dma_start(table_t[:, g * TC:(g + 1) * TC, 0:D],
                                 XN[:, g * TC:(g + 1) * TC, :]).then_inc(xn_stored, 16)
                if f == 0:
                    for q in range(WR):
                        load_weights(f, q)
                sp.wait_ge(gates_ready, f + 1)
                sp.dma_start(table_t[:, :, D:XGW], tB.rearrange("p (t e) -> p t e", e=E)).then_inc(gates_stored, 16)
                sp.wait_ge(list_split, f + 1)
                sp.dma_start(lst[0:CAP, CAP:P], lst[CAP:P, 0:CAP]).then_inc(list_joined, 16)
                for q in range(WR if f == 0 else 0, E // EW):
                    load_weights(f, q)
                if f == 0:
                    pass
                for g in range(NC):
                    n = f * NC + g
                    b = n % 2
                    for c in range(CHAINS):
                        sp.wait_ge(scattered[c], 16 * (f + 1) * (NP // CHAINS))
                    if g >= 2:
                        sp.wait_ge(plane_used, n - 1)
                    elif f == 0:
                        pass
                    for c in range(CHAINS):
                        sp.dma_start(PL[:, b, :, 2 * c:2 * c + 2, :],
                                     plane_t[c][:, g * TC:(g + 1) * TC, :].rearrange("p t (c d) -> p t c d", c=2)
                                     ).then_inc(plane_loaded[b], 16)
                if f == 0:
                    pass
            for g in range(NC):
                sp.wait_ge(x_final, g + 1)
                sp.dma_start(out_t[:, g * TC:(g + 1) * TC, :], X[:, g * TC:(g + 1) * TC, :]).then_inc(out_stored, 16)
            sp.wait_ge(out_stored, 16 * NC)

        @block.gpsimd
        def _(pool):
            pool.memset(mh[:, :], -0.5).then_inc(const_made, 1)
            pool.memset(zero[:, :], 0.0).then_inc(const_made, 1)
            pool.memset(XG[:, :, :], 0.0).then_inc(const_made, 1)
            pool.wait_ge(const_made, 3)

            def roots(ln, g):
                pool.wait_ge(mean_var, ln * NC + g + 1)
                pool.tensor_tensor(rstd[:, g * TC:(g + 1) * TC], mv[:, g * TC:(g + 1) * TC, 1], mh[:, :],
                                   ALU.pow).then_inc(rstd_ready, 1)

            def clear_planes(f):
                for c in range(CHAINS):
                    if f:
                        for b in range(2):
                            pool.wait_ge(plane_loaded[b], 16 * CHAINS * (NC // 2))
                    dst = planes[c][:, :].rearrange("(p r) d -> p (r d)", p=P).rearrange("p (n k) -> p n k", k=512)
                    pool.dma_start(dst, zero[:, None, :].to_broadcast([P, YR * D // P // 512, 512])
                                   ).then_inc(planes_zero[c], 16)

            for g in range(NC):
                roots(0, g)
            for f in range(2):
                clear_planes(f)
                pool.wait_ge(idx_ready, f + 1)
                pool.wait_ge(xn_stored, 16 * NC * (f + 1))
                pool.wait_ge(gates_stored, 16 * (f + 1))

                def gather(i):
                    n = f * NP + i
                    if n >= 8:
                        pool.wait_ge(*full(T_full, T_ex[f] + i - 8) if i >= 8 else full(T_full, T_ex[0] + NP - 8 + i))
                        pool.wait_ge(gc_ready, n - 7)
                    pool.indirect_dma_start(XG[:, n % 8, :], None, table[:, :],
                                            bass.IndirectOffsetOnAxis(ap=gidx[:, i:i + 1], axis=0),
                                            bounds_check=T - 1, oob_is_err=False).then_inc(gathered[n % 8], 16)

                for i in range(8):
                    gather(i)
                for c in range(CHAINS):
                    pool.wait_ge(planes_zero[c], 16 * (f + 1))
                for i in range(NP):
                    n = f * NP + i
                    pool.wait_ge(yo_ready, n + 1)
                    c = i % CHAINS
                    m = f * (NP // CHAINS) + i // CHAINS
                    if m:
                        pool.wait_ge(scattered[c], 16 * m)
                    pool.indirect_dma_start(planes[c][:, :], bass.IndirectOffsetOnAxis(ap=sidx[:, i:i + 1], axis=0),
                                            YO[:, n % 4, :], None, bounds_check=YR - 1, oob_is_err=True,
                                            compute_op=ALU.add).then_inc(scattered[c], 16)
                    if i + 8 < NP:
                        gather(i + 8)
                if f == 0:
                    for ln in (1, 2):
                        for g in range(NC):
                            roots(ln, g)

        @block.tensor
        def _(pe):
            pe.wait_ge(const_loaded, 16 * 10)

            def layernorm_T(ln, g, logits):
                pe.wait_ge(xn_ready, ln * NC + g + 1)
                for q in range(g * TC // 2, (g + 1) * TC // 2):
                    n = T_ln[ln] + q
                    if n >= 2:
                        pe.wait_ge(T_free[n % 2], n // 2)
                    for j in range(2):
                        for k in range(KD):
                            mm = pe.transpose(psT[n % 2][:, k * 2 * P + j * P:k * 2 * P + (j + 1) * P],
                                              XN[:, 2 * q + j, k * P:(k + 1) * P], ident)
                    mm.then_inc(T_full[n % 2], 1)

            def logits(f, g):
                for q in range(g * TC // 2, (g + 1) * TC // 2):
                    pe.wait_ge(xt_ready, 2 * f * NPAIR + q + 1)
                    for j in (2 * q, 2 * q + 1):
                        for k in range(KD):
                            mm = pe.matmul(psR[j // 8][:, j % 8 * E:(j % 8 + 1) * E], XT[:, k, j * P:(j + 1) * P],
                                           gw[:, k, :], start=(k == 0), stop=(k == KD - 1))
                    mm.then_inc(logits_ready, 1)

            def up(f, c):
                for h in range(HB):
                    n = A_up[f] + c * HB + h
                    if n >= 2:
                        pe.wait_ge(A_free[n % 2], n // 2)
                    for k in range(KD):
                        mm = pe.matmul(psA[n % 2][:, :], su[:, k, h * P:(h + 1) * P], XT[:, k, c * CH:(c + 1) * CH],
                                       start=(k == 0), stop=(k == KD - 1))
                    mm.then_inc(A_full[n % 2], 1)

            def down(f, c):
                pe.wait_ge(hid_ready, f * UP + (c + 1) * HB)
                for q in range(TC // 2):
                    n = C_dn[f] + c * TC // 2 + q
                    if n >= 2:
                        pe.wait_ge(C_free[n % 2], n // 2)
                    for j in range(2):
                        tt = (2 * q + j) * P
                        for h in range(HB):
                            mm = pe.matmul(psC[n % 2][:, j * D:(j + 1) * D], HID[:, c % 2, h, tt:tt + P], sd[:, h, :],
                                           start=(h == 0), stop=(h == HB - 1))
                    mm.then_inc(C_full[n % 2], 1)

            def mask_T(f):
                pe.wait_ge(mask_ready, f + 1)
                pb = psR[0][:, :].bitcast(BF16)
                for t in range(NT // 2):
                    mm = pe.transpose(pb[:, t * P:(t + 1) * P], maskb[:, t, :, :].rearrange("p h e -> p (h e)"), identb[:, :])
                mm.then_inc(maskT_ready, 1)

            def key_slots(f):
                pe.wait_ge(slots_ready, f + 1)
                for h in range(2):
                    mm = pe.matmul(psR[1][h * CAP:(h + 1) * CAP, 0:NP], lstB[0:E, 0:CAP], sel[0:E, h * NP:(h + 1) * NP],
                                   start=True, stop=True)
                mm.then_inc(keyslot_ready, 1)

            def turn(f, i):
                n = f * NP + i
                pe.wait_ge(gathered[n % 8], 16 * (n // 8 + 1))
                u = T_ex[f] + i
                pe.wait_ge(T_free[u % 2], u // 2)
                for k in range(KD):
                    mm = pe.transpose(psT[u % 2][:, k * P:(k + 1) * P], XG[:, n % 8, k * P:(k + 1) * P], ident)
                mm.then_inc(T_full[u % 2], 1)

            def first(f, i):
                n = f * NP + i
                w = (n * 2) // EW
                pe.wait_ge(w_loaded[w % WR], 16 * (w // WR + 1))
                pe.wait_ge(xd_ready, n + 1)
                u = A_ex[f] + i
                pe.wait_ge(A_free[u % 2], u // 2)
                for s in range(2):
                    e = (2 * i + s) % EW
                    for k in range(KD):
                        mm = pe.matmul(psA[u % 2][:, s * CAP:(s + 1) * CAP], W[:, w % WR, e, k * I:(k + 1) * I],
                                       XD[:, n % 3, k, s * CAP:(s + 1) * CAP], start=(k == 0), stop=(k == KD - 1))
                mm.then_inc(A_full[u % 2], 1)

            def second(f, i):
                n = f * NP + i
                w = (n * 2) // EW
                pe.wait_ge(h_ready, n + 1)
                u = C_ex[f] + i
                pe.wait_ge(C_free[u % 2], u // 2)
                for s in range(2):
                    e = (2 * i + s) % EW
                    mm = pe.matmul(psC[u % 2][s * CAP:(s + 1) * CAP, 0:D], HT2[:, n % 3, s * CAP:(s + 1) * CAP],
                                   W[:, w % WR, e, KD * I:], start=True, stop=True)
                mm.then_inc(C_full[u % 2], 1)
                pe.wait_ge(C_full[u % 2], u // 2 + 1)
                pe.nop().then_inc(mm2_done, 1)

            def ffn(f):
                up(f, 0)
                up(f, 1)
                mask_T(f)
                down(f, 0)
                up(f, 2)
                down(f, 1)
                up(f, 3)
                down(f, 2)
                down(f, 3)
                key_slots(f)
                for s in range(NP + 2):
                    if s < NP:
                        turn(f, s)
                    if 1 <= s <= NP:
                        first(f, s - 1)
                    if s >= 2:
                        second(f, s - 2)

            def attention(c):
                n = [A_att + c * ATT_A]

                def slot():
                    u = n[0]
                    n[0] += 1
                    pe.wait_ge(A_free[u % 2], u // 2)
                    return u
                for k in range(KD * (c == 0)):
                    pass
                pe.wait_ge(xt_ready, NPAIR + (c + 1) * TC // 2)
                u = slot()
                for k in range(KD):
                    mm = pe.matmul(psA[u % 2][0:DH, :], wg1s[:, k, :], XT[:, k, c * CH:(c + 1) * CH],
                                   start=(k == 0), stop=(k == KD - 1))
                mm.then_inc(A_full[u % 2], 1)
                pe.wait_ge(hA_ready, c + 1)
                for r in range(KD):
                    u = slot()
                    pe.matmul(psA[u % 2][:, :], wg2s[:, r * P:(r + 1) * P], hA[0:DH, :],
                              start=True, stop=True).then_inc(A_full[u % 2], 1)
                for w in (wus, wvs):
                    for r in range(KD):
                        u = slot()
                        for k in range(KD):
                            mm = pe.matmul(psA[u % 2][:, :], w[:, k, r * P:(r + 1) * P], XT[:, k, c * CH:(c + 1) * CH],
                                           start=(k == 0), stop=(k == KD - 1))
                        mm.then_inc(A_full[u % 2], 1)

            def att_project(c):
                pe.wait_ge(go_ready, c + 1)
                pe.wait_ge(cv_ready, c + 1)
                for q in range(TC // 2):
                    u = C_att + c * TC // 2 + q
                    pe.wait_ge(C_free[u % 2], u // 2)
                    for j in range(2):
                        tt = (2 * q + j) * P
                        for k in range(KD):
                            pe.matmul(psC[u % 2][:, j * D + k * P:j * D + (k + 1) * P],
                                      cv[:, c % 2, k, tt:tt + P], ident, start=(k == 0), stop=False)
                        for r in range(KD):
                            mm = pe.matmul(psC[u % 2][:, j * D:(j + 1) * D], go[:, c % 2, r, tt:tt + P],
                                           wus[:, r, :], start=False, stop=(r == KD - 1))
                    mm.then_inc(C_full[u % 2], 1)

            pe.wait_ge(dve_step, 1)
            for g in range(NC):
                layernorm_T(0, g, True)
                logits(0, g)
            ffn(0)
            for g in range(NC):
                layernorm_T(1, g, False)
            for c in range(NC + 2):
                if c < NC:
                    attention(c)
                if 1 <= c <= NC:
                    att_project(c - 1)
                if c >= 2:
                    layernorm_T(2, c - 2, True)
                    logits(1, c - 2)
            ffn(1)

        @block.scalar
        def _(act):
            steps = [0]

            def link(ins):
                steps[0] += 1
                ins.then_inc(act_step, 1)
                act.wait_ge(act_step, steps[0])

            act.wait_ge(const_loaded, 16 * 10)

            def xt_copy(ln, g):
                for q in range(g * TC // 2, (g + 1) * TC // 2):
                    n = T_ln[ln] + q
                    act.wait_ge(*full(T_full, n))
                    act.activation(XT[:, :, q * 2 * P:(q + 1) * 2 * P],
                                   psT[n % 2][:, :].rearrange("p (k t) -> p k t", k=KD), ACT.Copy).then_inc(xt_ready, 1)
                    act.wait_ge(xt_ready, ln * NPAIR + q + 1)
                    act.nop().then_inc(T_free[n % 2], 1)

            def hidden(f, c):
                for h in range(HB):
                    n = A_up[f] + c * HB + h
                    act.wait_ge(*full(A_full, n))
                    if h == 0 and f * NC + c >= 2:
                        pass
                    link(act.activation(HID[:, c % 2, h, :], psA[n % 2][:, :], ACT.Relu))
                    act.nop().then_inc(A_free[n % 2], 1)
                    act.activation(HID[:, c % 2, h, :], HID[:, c % 2, h, :], ACT.Square).then_inc(hid_ready, 1)

            def shared_out(f, c):
                for q in range(TC // 2):
                    n = C_dn[f] + c * TC // 2 + q
                    act.wait_ge(*full(C_full, n))
                    j = c * TC + 2 * q
                    link(act.activation(S[:, j:j + 2, :], psC[n % 2][:, :].rearrange("p (t d) -> p t d", d=D),
                                        ACT.Copy, scale=HALF))
                    act.nop().then_inc(C_free[n % 2], 1)
                act.nop().then_inc(shared_ready, 1)

            def ffn(f):
                act.wait_ge(logits_ready, (f + 1) * NPAIR)
                for h in range(2):
                    ins = act.activation(sco[:, h * 8:(h + 1) * 8, :],
                                         psR[h][:, :].rearrange("p (t e) -> p t e", e=E), ACT.Sigmoid)
                    ins.then_inc(scores_ready, 1)
                hidden(f, 0)
                hidden(f, 1)
                shared_out(f, 0)
                hidden(f, 2)
                shared_out(f, 1)
                hidden(f, 3)
                shared_out(f, 2)
                shared_out(f, 3)

                def relu(i):
                    n = f * NP + i
                    u = A_ex[f] + i
                    act.wait_ge(*full(A_full, u))
                    if n >= 3:
                        act.wait_ge(h_ready, n - 2)
                    act.activation(RH[:, n % 3, :], psA[u % 2][:, 0:P], ACT.Relu).then_inc(relu_ready, 1)
                    act.wait_ge(relu_ready, n + 1)
                    act.nop().then_inc(A_free[u % 2], 1)

                def gated(i):
                    n = f * NP + i
                    u = C_ex[f] + i
                    act.wait_ge(*full(C_full, u))
                    act.wait_ge(gc_ready, n + 1)
                    if n >= 4:
                        m = (n - 4) // CHAINS + 1
                        act.wait_ge(scattered[i % CHAINS], 16 * m)
                    act.activation(YO[:, n % 4, :], psC[u % 2][:, 0:D], ACT.Copy, scale=GC[:, n % 4:n % 4 + 1]
                                   ).then_inc(yo_ready, 1)
                    act.wait_ge(yo_ready, n + 1)
                    act.nop().then_inc(C_free[u % 2], 1)

                for s in range(NP + 1):
                    if s < NP:
                        relu(s)
                    if s >= 1:
                        gated(s - 1)

            def attention(c):
                n = A_att + c * ATT_A
                act.wait_ge(*full(A_full, n))
                act.activation(hA[0:DH, :], psA[n % 2][0:DH, :], ACT.Relu, bias=bg1).then_inc(hA_ready, 1)
                act.wait_ge(hA_ready, c + 1)
                act.nop().then_inc(A_free[n % 2], 1)
                for k in range(KD):
                    if c >= 2 and k == 0:
                        act.wait_ge(*full(C_full, C_att + (c - 1) * TC // 2 - 1))
                    act.activation(cv[:, c % 2, k, :], XT[:, k, c * CH:(c + 1) * CH], ACT.Identity,
                                   bias=cb[:, k:k + 1], scale=cw1[:, k:k + 1]).then_inc(cv_first, 1)
                if c >= 1:
                    act.wait_ge(uv_used, 4 * c)
                for r in range(KD):
                    u = n + 1 + r
                    act.wait_ge(*full(A_full, u))
                    act.activation(gT[:, r, :], psA[u % 2][:, :], ACT.Sigmoid, bias=bg2[:, r:r + 1]).then_inc(gT_ready, 1)
                    act.wait_ge(gT_ready, c * KD + r + 1)
                    act.nop().then_inc(A_free[u % 2], 1)

            for g in range(NC):
                xt_copy(0, g)
            ffn(0)
            for g in range(NC):
                xt_copy(1, g)
            for c in range(NC + 2):
                if c < NC:
                    attention(c)
                if c >= 2:
                    xt_copy(2, c - 2)
            ffn(1)

        @block.vector
        def _(dve):
            steps = [0]

            def link(ins):
                steps[0] += 1
                ins.then_inc(dve_step, 1)
                dve.wait_ge(dve_step, steps[0])

            def stats(ln, g):
                for j in range(g * TC, (g + 1) * TC):
                    ins = dve.bn_stats(st[:, j, :], X[:, j, :])
                link(ins)
                for j in range(g * TC, (g + 1) * TC):
                    ins = dve.bn_aggr(mv[:, j, :], st[:, j, :])
                link(ins)
                s = mv[:, g * TC:(g + 1) * TC, 1]
                dve.tensor_scalar(s, s, EPS, None, ALU.add).then_inc(mean_var, 1)

            def normal(ln, g):
                dve.wait_ge(rstd_ready, ln * NC + g + 1)
                dve.wait_ge(mean_var, ln * NC + g + 1)
                if ln:
                    n = T_ln[ln - 1] + (g + 1) * TC // 2 - 1
                    dve.wait_ge(*full(T_full, n))
                    if ln == 1:
                        dve.wait_ge(xn_stored, 16 * NC)
                for j in range(g * TC, (g + 1) * TC):
                    ins = dve.tensor_scalar(XN[:, j, :], X[:, j, :], mv[:, j, 0:1], rstd[:, j:j + 1],
                                            ALU.subtract, ALU.mult)
                ins.then_inc(xn_ready, 1)

            link(dve.memset(msk[:, :, E:E + 2], 2 * FAR))
            dve.wait_ge(const_loaded, 16 * 10)
            link(dve.tensor_copy(identb[:, :], ident))

            def router(f):
                v4 = lambda a: a.rearrange("p (t g s) -> p (t g) s", g=NGRP, s=GS)
                dve.wait_ge(scores_ready, 2 * f + 2)
                link(dve.memset(msk[:, :, E:E + 2], 2 * FAR))
                link(dve.tensor_tensor(scb[:, :, :], sco[:, :, :], eb[:, None, :].to_broadcast([P, NT, E]), ALU.add))
                a = scb[:, :, :].rearrange("p t (g s) -> p (t g) s", s=GS)
                NG = NT * NGRP
                q = NG * 4
                hi = tA[:, 0:q].rearrange("p (g s) -> p g s", s=4)
                lo = tA[:, q:2 * q].rearrange("p (g s) -> p g s", s=4)
                dve.tensor_tensor(hi, a[:, :, 0:4], a[:, :, 4:8], ALU.max)
                link(dve.tensor_tensor(lo, a[:, :, 0:4], a[:, :, 4:8], ALU.min))
                q = NG * 2
                h2 = tB[:, 0:q].rearrange("p (g s) -> p g s", s=2)
                m2 = tB[:, q:2 * q].rearrange("p (g s) -> p g s", s=2)
                l2 = tC[:, 0:q].rearrange("p (g s) -> p g s", s=2)
                n2 = tC[:, q:2 * q].rearrange("p (g s) -> p g s", s=2)
                dve.tensor_tensor(h2, hi[:, :, 0:2], hi[:, :, 2:4], ALU.max)
                dve.tensor_tensor(m2, hi[:, :, 0:2], hi[:, :, 2:4], ALU.min)
                link(dve.tensor_tensor(l2, lo[:, :, 0:2], lo[:, :, 2:4], ALU.max))
                link(dve.tensor_tensor(n2, m2, l2, ALU.max))
                h1, m1, l1, n1 = (tA[:, NG * z:NG * (z + 1)] for z in range(4))
                dve.tensor_tensor(h1, h2[:, :, 0], h2[:, :, 1], ALU.max)
                dve.tensor_tensor(m1, h2[:, :, 0], h2[:, :, 1], ALU.min)
                link(dve.tensor_tensor(l1, n2[:, :, 0], n2[:, :, 1], ALU.max))
                link(dve.tensor_tensor(n1, m1, l1, ALU.max))
                link(dve.tensor_tensor(gsc[:, :, :].rearrange("p t g -> p (t g)"), h1, n1, ALU.add))
                B = [P, NT, NGRP, NGRP]
                other = gsc[:, :, None, :].to_broadcast(B)
                mine = gsc[:, :, :, None].to_broadcast(B)
                g4 = lambda z: z.rearrange("p (t g s) -> p t g s", g=NGRP, s=NGRP)
                low = lower.rearrange("p (g s) -> p g s", s=NGRP)
                dve.tensor_tensor(g4(tA), other, mine, ALU.is_gt)
                link(dve.tensor_tensor(g4(tB), other, mine, ALU.is_equal))
                link(dve.tensor_tensor(g4(tB), g4(tB), low[:, None, :, :].to_broadcast(B), ALU.mult))
                link(dve.tensor_tensor(tA, tA, tB, ALU.add))
                link(dve.tensor_reduce(gpen[:, :, :], g4(tA), AX.X, ALU.add))
                link(dve.tensor_scalar(gpen[:, :, :], gpen[:, :, :], TOPG - 0.5, -FAR, ALU.is_gt, ALU.mult))
                link(dve.tensor_tensor(msk[:, :, 0:E].rearrange("p t (g s) -> p t g s", s=GS),
                                       scb[:, :, :].rearrange("p t (g s) -> p t g s", s=GS),
                                       gpen[:, :, :, None].to_broadcast([P, NT, NGRP, GS]), ALU.add))
                for t in range(NT):
                    ins = dve.max(top[:, t, :], msk[:, t, 0:E])
                link(ins)
                link(dve.memset(top[:, :, TOPK:8], 2 * FAR))
                for t in range(NT):
                    ins = dve.match_replace(rep[:, t, :], top[:, t, :], msk[:, t, :], FAR)
                link(ins)
                dve.tensor_scalar(maskb[:, :, :, :].rearrange("p t h e -> p h t e"),
                                  rep[:, :, 0:E].rearrange("p (h t) e -> p h t e", h=2), FAR, None, ALU.is_equal).then_inc(mask_ready, 1)
                link(dve.tensor_scalar(tA.rearrange("p (t e) -> p t e", e=E), rep[:, :, 0:E], FAR, None, ALU.is_equal))
                link(dve.tensor_tensor(tC, tA, sco[:, :, :].rearrange("p t e -> p (t e)"), ALU.mult))
                t3 = lambda z: z.rearrange("p (t e) -> p t e", e=E)
                link(dve.tensor_reduce(wsum, t3(tC), AX.X, ALU.add))
                link(dve.tensor_scalar(wsum, wsum, 1e-20, None, ALU.add))
                link(dve.reciprocal(wrec, wsum))
                link(dve.tensor_scalar(wrec, wrec, ROUTE_SCALE * HALF, None, ALU.mult))
                dve.tensor_tensor(t3(tB), t3(tC), wrec[:, :, None].to_broadcast([P, NT, E]), ALU.mult
                                  ).then_inc(gates_ready, 1)
                dve.wait_ge(maskT_ready, f + 1)
                link(dve.tensor_tensor(keyA, psR[0][:, :].bitcast(BF16), keyrow, ALU.mult))
                a, b = keyA, keyB
                for r in range(CAP // 8):
                    link(dve.max(lst[:, r * 8:(r + 1) * 8], a))
                    if r < CAP // 8 - 1:
                        link(dve.match_replace(b, lst[:, r * 8:(r + 1) * 8], a, 0.0))
                        a, b = b, a
                dve.nop().then_inc(list_split, 1)
                dve.wait_ge(list_joined, 16 * (f + 1))
                a, b = lst, lstA
                for r in range(CAP // 8):
                    link(dve.max(lstB[0:CAP, r * 8:(r + 1) * 8], a[0:CAP, :]))
                    if r < CAP // 8 - 1:
                        link(dve.match_replace(b[0:CAP, :], lstB[0:CAP, r * 8:(r + 1) * 8], a[0:CAP, :], 0.0))
                        a, b = b, a
                dve.nop().then_inc(slots_ready, 1)
                dve.wait_ge(keyslot_ready, f + 1)
                tok, emp = tA[:, 0:NP], tA[:, NP:2 * NP]
                key = psR[1][:, 0:NP]
                dve.tensor_scalar(gidx[:, :], key, -1.0, float(T), ALU.mult, ALU.add)
                dve.tensor_scalar(tok, key, -2.0, 2.0 * T, ALU.mult, ALU.add)
                link(dve.tensor_scalar(emp, key, 0.0, slotno, ALU.is_equal, ALU.mult))
                link(dve.tensor_tensor(tok, tok, emp, ALU.add))
                link(dve.tensor_scalar(sidx[:, :], tok, half, None, ALU.add))
                dve.nop().then_inc(idx_ready, 1)

            def experts(f):
                def xd(i):
                    n = f * NP + i
                    u = T_ex[f] + i
                    dve.wait_ge(*full(T_full, u))
                    if n >= 3:
                        m = A_ex[f] + i - 3 if i >= 3 else A_ex[0] + NP - 3 + i
                        dve.wait_ge(*full(A_full, m))
                    dve.tensor_copy(XD[:, n % 3, :, :], psT[u % 2][:, 0:D].rearrange("p (k s) -> p k s", k=KD)
                                    ).then_inc(xd_ready, 1)
                    if n >= 4:
                        dve.wait_ge(yo_ready, n - 3)
                    dve.tensor_tensor_reduce(out=GJ[:, n % 4, :], in0=XG[:, n % 8, D + 2 * i:D + 2 * i + 2], in1=parity,
                                             scale=1.0, scalar=0.0, op0=ALU.mult, op1=ALU.add,
                                             accum_out=GC[:, n % 4:n % 4 + 1]).then_inc(gc_ready, 1)
                    dve.wait_ge(xd_ready, n + 1)
                    dve.nop().then_inc(T_free[u % 2], 1)

                def square(i):
                    n = f * NP + i
                    dve.wait_ge(relu_ready, n + 1)
                    if n >= 3:
                        m = C_ex[f] + i - 3 if i >= 3 else C_ex[0] + NP - 3 + i
                        dve.wait_ge(*full(C_full, m))
                    dve.tensor_tensor(HT2[:, n % 3, :], RH[:, n % 3, :], RH[:, n % 3, :], ALU.mult).then_inc(h_ready, 1)

                for s in range(NP + 1):
                    if s < NP:
                        xd(s)
                    if s >= 1:
                        square(s - 1)

            def combine(f, g):
                n = f * NC + g
                b = n % 2
                gs = slice(g * TC, (g + 1) * TC)
                dve.wait_ge(shared_ready, f * NC + g + 1)
                link(dve.tensor_tensor(X[:, gs, :], X[:, gs, :], S[:, gs, :], ALU.add))
                dve.wait_ge(plane_loaded[b], 16 * CHAINS * (n // 2 + 1))
                for c in range(2 * CHAINS):
                    ins = dve.tensor_tensor(X[:, gs, :], X[:, gs, :], PL[:, b, :, c, :], ALU.add)
                    if c < 2 * CHAINS - 1 or f == 0:
                        link(ins)
                if f:
                    ins.then_inc(x_final, 1)
                    dve.wait_ge(x_final, g + 1)
                dve.nop().then_inc(plane_used, 1)

            def attention(c):
                n = A_att + c * ATT_A
                dve.wait_ge(gT_ready, KD * (c + 1))
                for z, (dst, b) in enumerate(((ug, bu), (vg, bv))):
                    for r in range(KD):
                        u = n + 1 + KD + z * KD + r
                        dve.wait_ge(*full(A_full, u))
                        link(dve.scalar_tensor_tensor(out=dst[:, r, :], in0=psA[u % 2][:, :], scalar=b[:, r:r + 1],
                                                      in1=gT[:, r, :], op0=ALU.add, op1=ALU.mult))
                        dve.nop().then_inc(A_free[u % 2], 1)
                        dve.nop().then_inc(uv_used, 1)
                for r in range(KD):
                    for s in range(SEQ):
                        ins = dve.tensor_tensor_scan(cum[:, r, s * L:(s + 1) * L], ones, ug[:, r, s * L:(s + 1) * L],
                                                     0.0, ALU.mult, ALU.add)
                link(ins)
                if c >= 2:
                    dve.wait_ge(*full(C_full, C_att + (c - 1) * TC // 2 - 1))
                dve.tensor_tensor(go[:, c % 2, :, :], cum[:, :, :], vg[:, :, :], ALU.mult).then_inc(go_ready, 1)
                dve.wait_ge(cv_first, KD * (c + 1))
                for k in range(KD):
                    xv = XT[:, k, c * CH:(c + 1) * CH].rearrange("p (s l) -> p s l", l=L)
                    t = cv[:, c % 2, k, :].rearrange("p (s l) -> p s l", l=L)
                    link(dve.scalar_tensor_tensor(out=t[:, :, 1:L], in0=xv[:, :, 0:L - 1], scalar=cw0[:, k:k + 1],
                                                  in1=t[:, :, 1:L], op0=ALU.mult, op1=ALU.add))
                    link(dve.scalar_tensor_tensor(out=t[:, :, 0:L - 1], in0=xv[:, :, 1:L], scalar=cw2[:, k:k + 1],
                                                  in1=t[:, :, 0:L - 1], op0=ALU.mult, op1=ALU.add))
                dve.nop().then_inc(cv_ready, 1)

            def att_residual(c):
                for q in range(TC // 2):
                    u = C_att + c * TC // 2 + q
                    j = c * TC + 2 * q
                    dve.wait_ge(*full(C_full, u))
                    link(dve.tensor_tensor(X[:, j:j + 2, :], X[:, j:j + 2, :],
                                           psC[u % 2][:, :].rearrange("p (t d) -> p t d", d=D), ALU.add))
                    dve.nop().then_inc(C_free[u % 2], 1)

            for g in range(NC):
                dve.wait_ge(x_loaded[g], 16)
                stats(0, g)
                if g:
                    normal(0, g - 1)
            normal(0, NC - 1)
            router(0)
            experts(0)
            for g in range(NC):
                combine(0, g)
                stats(1, g)
                if g:
                    normal(1, g - 1)
            normal(1, NC - 1)
            for c in range(NC + 1):
                if c < NC:
                    attention(c)
                if c >= 1:
                    att_residual(c - 1)
                    stats(2, c - 1)
                    normal(2, c - 1)
            router(1)
            experts(1)
            for g in range(NC):
                combine(1, g)


def kernel(L0_attn_x, L0_attn_Wu, L0_attn_bu, L0_attn_Wv, L0_attn_bv, L0_attn_Wg1, L0_attn_bg1, L0_attn_Wg2,
           L0_attn_bg2, L0_attn_conv_w, L0_attn_conv_b, L0_ffn_gate_w, L0_ffn_e_bias, L0_ffn_w1, L0_ffn_w2,
           L0_ffn_shared_up_w, L0_ffn_shared_down_w):
    import numpy as np
    import concourse.bacc as bacc
    from concourse.bass_utils import run_bass_kernel_spmd

    def blocks(w):
        w = np.asarray(w)
        return np.ascontiguousarray(w.reshape(-1, P, w.shape[1]).transpose(1, 0, 2))

    x = np.asarray(L0_attn_x)
    B, L, D = x.shape
    T = B * L
    w1, w2 = np.asarray(L0_ffn_w1), np.asarray(L0_ffn_w2)
    E, I, _ = w1.shape
    KD = D // P
    w1l = w1.transpose(2, 0, 1).reshape(KD, P, E, I).transpose(1, 2, 0, 3).reshape(P, E, KD * I)
    w2l = w2.transpose(2, 0, 1)
    wexp = np.ascontiguousarray(np.concatenate([w1l, w2l], axis=2))
    col = lambda v: np.asarray(v).reshape(KD, P).T
    cw = np.asarray(L0_attn_conv_w)[:, 0, :]
    bg1 = np.asarray(L0_attn_bg1)
    vecs = np.ascontiguousarray(np.concatenate(
        [col(L0_attn_bu), col(L0_attn_bv), col(L0_attn_bg2), col(L0_attn_conv_b),
         col(cw[:, 0]), col(cw[:, 1]), col(cw[:, 2]),
         np.pad(bg1, (0, P - bg1.size)).reshape(P, 1)], axis=1))
    p = np.arange(P)
    lower = (np.arange(NGRP)[None, :] < np.arange(NGRP)[:, None]).astype(np.float32)
    NP = E // 2
    sel = np.zeros((P, 2, NP), np.float32)
    for e in range(E):
        sel[e, e % 2, e // 2] = 1
    keyrow = T - (p[:, None] // E * (T // 2) + np.arange(T // 2)[None, :])
    consts = np.ascontiguousarray(np.concatenate(
        [np.eye(P), np.broadcast_to(lower.reshape(1, -1), (P, NGRP * NGRP)), np.ones((P, L)),
         np.stack([p < CAP, p >= CAP], 1), (p >= CAP)[:, None], p[:, None], sel.reshape(P, -1), keyrow],
        axis=1).astype(np.float32))
    arrays = {
        "x": np.ascontiguousarray(x.reshape(T, D)), "wexp": wexp,
        "gate": blocks(np.asarray(L0_ffn_gate_w).T),
        "ebias": np.ascontiguousarray(np.broadcast_to(np.asarray(L0_ffn_e_bias)[None, :], (P, E))),
        "sup": blocks(np.asarray(L0_ffn_shared_up_w).T), "sdown": blocks(np.asarray(L0_ffn_shared_down_w).T),
        "wu": blocks(np.asarray(L0_attn_Wu).T), "wv": blocks(np.asarray(L0_attn_Wv).T),
        "wg1": blocks(np.asarray(L0_attn_Wg1).T), "wg2": np.ascontiguousarray(np.asarray(L0_attn_Wg2).T),
        "vecs": vecs, "consts": consts,
    }
    nc = bacc.Bacc("TRN2", target_bir_lowering=False, num_devices=1)
    args = [nc.dram_tensor(n, a.shape, mybir.dt.from_np(a.dtype), kind="ExternalInput").ap() for n, a in arrays.items()]
    out = nc.dram_tensor("out", (T, D), F32, kind="ExternalOutput").ap()
    build(nc, *args, out)
    r = run_bass_kernel_spmd(nc, [arrays], core_ids=[0])
    return r.results[0]["out"].reshape(B, L, D)
```

```python
from contextlib import ExitStack

import concourse.bass as bass
from concourse import mybir

ALU = mybir.AluOpType
ACT = mybir.ActivationFunctionType
AX = mybir.AxisListType
F32 = mybir.dt.float32
BF16 = mybir.dt.bfloat16
F16 = mybir.dt.float16
U32 = mybir.dt.uint32

P = 128
EPS = 1e-5
TOPK = 6
NGRP = 8
TOPG = 4
CAP = 64
ROUTE_SCALE = 2.5
HALF = 0.5
FAR = 1e30


PASSES = ((0, 0), (1, 0), (0, 1))


def build(nc, x, wexp, ebias, wsplit, sdown, wu, wg2, convb, vecs, consts, keys, out):
    T, D = x.shape
    NT = T // P
    KD = D // P
    E = wexp.shape[1]
    I = P
    SH = sdown.shape[1] * P
    HB = SH // P
    GS = E // NGRP
    NP = E // 2
    assert 2 * CAP == P
    CH = 512
    NC = T // CH
    TC = CH // P
    L = 256
    SEQ = CH // L
    DH = wg2.shape[0]
    HT = T // 2
    CHAINS = 2
    WR = 7
    SR = 4
    XR = 8
    SW = L + 2
    XGW = D + E
    NLN = 3

    with ExitStack() as ctx:
        def sb(name, shape, dt=F32):
            return ctx.enter_context(nc.sbuf_tensor(name, shape, dt))

        def sem(name):
            return ctx.enter_context(nc.semaphore(name))

        X = sb("X", [P, NT, D])
        XF = sb("XF", [P, TC, D])
        XN = sb("XN", [P, NT, 2, D], F16)
        XT = sb("XT", [P, 2, KD, T // L * SW + 2], F16)
        S = sb("S", [P, 2, 2 * D])
        HID = sb("HID", [P, 2, HB, CH])
        W = sb("W", [P, WR, 2, KD * I + D])
        W1 = sb("W1", [P, SR, 2, 2, KD * I], F16)
        XG = sb("XG", [P, XR, XGW])
        XD = sb("XD", [P, 3, 2 * KD * P], F16)
        RH = sb("RH", [P, 3, P])
        HT2 = sb("HT2", [P, 3, P])
        YO = sb("YO", [P, 4, D])
        GC = sb("GC", [P, 4])
        GJ = sb("GJ", [P, 4, 2])
        SCR = sb("SCR", [P, 10112])
        raw = HID[:, :, :, :].rearrange("p a b c -> p (a b c)")[:, 0:wsplit.shape[1] + 3 * KD * P]
        w16 = sb("w16", [P, 2, raw.shape[1]], F16)
        sd = sb("sd", [P, HB, D])
        eb = sb("eb", [P, E])
        wus = sb("wus", [P, KD, D])
        cbs = sb("cbs", [1, D])
        cb16 = sb("cb16", [1, 2, D], F16)
        one16 = sb("one16", [1, P], F16)
        wg2s = sb("wg2s", [DH, D])
        vec = sb("vec", [P, vecs.shape[1]])
        cst = sb("cst", [P, consts.shape[1]])
        st = sb("st", [P, NT, 6])
        mv = sb("mv", [P, NT, 2])
        rstd = sb("rstd", [P, NT])
        mh = sb("mh", [P, TC])
        negmean = sb("negmean", [P, NT])
        shift = sb("shift", [P, NT])
        maskb = sb("maskb", [P, NT // 2, 2, E], BF16)
        identb = sb("identb", [P, P], BF16)
        ident16 = sb("ident16", [P, P], F16)
        keyrow = sb("keyrow", [P, HT])
        gidx = sb("gidx", [P, NP], U32)
        sidx = sb("sidx", [P, NP], U32)
        zero = sb("zero", [P, 256])

        o = 0
        def cut(n):
            nonlocal o
            o += n
            return cst[:, o - n:o]
        ident = cut(P)
        lower = cut(NGRP * NGRP)
        ones = cut(L)
        parity = cut(2)
        half = cut(1)
        slotno = cut(1)
        sel = cut(2 * NP)
        bu, bv, bg2 = (vec[:, KD * i:KD * (i + 1)] for i in range(3))
        cw = [vec[:, KD * i:KD * (i + 1)] for i in range(3, 6)]
        bg1 = vec[0:DH, 6 * KD:6 * KD + 1]

        o = 0
        def half_of(n):
            nonlocal o
            o += KD * n
            return w16[:, :, o - KD * n:o].rearrange("p h (k n) -> p h k n", k=KD)
        gw, su, wu16, wv16, wg16 = half_of(E), half_of(SH), half_of(D), half_of(D), half_of(DH)
        assert o == wsplit.shape[1]
        diag = w16[:, :, o:].rearrange("p h (j k n) -> p h j k n", j=3, k=KD)

        def tokens(half, k, t, n, shift=0):
            b = t // L * SW + 2 + t % L + shift
            if n <= L:
                return XT[:, half, k, b:b + n]
            return XT[:, half, k, b:b + n // L * SW].rearrange("p (s l) -> p s l", l=SW)[:, :, 0:L]

        at = 0
        def take(n):
            nonlocal at
            at += n
            return SCR[:, at - n:at]
        hA = take(CH)
        gT = take(KD * CH).rearrange("p (k t) -> p k t", k=KD)
        ug = take(KD * CH).rearrange("p (k t) -> p k t", k=KD)
        vg = take(KD * CH).rearrange("p (k t) -> p k t", k=KD)
        cum = take(KD * CH).rearrange("p (k t) -> p k t", k=KD)
        go = take(2 * KD * CH).rearrange("p (b k t) -> p b k t", b=2, k=KD)
        gates = take(NT * E).rearrange("p (t e) -> p t e", e=E)
        sco = take(TC * E).rearrange("p (t e) -> p t e", e=E)
        scb = take(TC * E).rearrange("p (t e) -> p t e", e=E)
        msk = take(TC * (E + 2)).rearrange("p (t e) -> p t e", e=E + 2)
        rept = take(TC * (E + 2)).rearrange("p (t e) -> p t e", e=E + 2)
        tA = take(TC * E)
        tB = take(TC * E)
        tC = take(TC * E)
        top = take(TC * 8).rearrange("p (t k) -> p t k", k=8)
        gsc = take(TC * NGRP).rearrange("p (t g) -> p t g", g=NGRP)
        gpen = take(TC * NGRP).rearrange("p (t g) -> p t g", g=NGRP)
        wsum = take(TC)
        wrec = take(TC)
        slot_a = take(NP)
        slot_b = take(NP)
        SCRW = at
        assert SCRW <= 10112
        at = 0
        keyA = take(HT)
        keyB = take(HT)
        lst = take(P)
        lstA = take(P)
        lstB = take(P)
        PL = SCR[:, 0:2 * TC * CHAINS * 2 * D].rearrange("p (b t c d) -> p b t c d", b=2, t=TC, d=D)

        psT = [ctx.enter_context(nc.psum_tensor(f"psT{b}", [P, 512], F32)) for b in range(2)]
        psA = [ctx.enter_context(nc.psum_tensor(f"psA{b}", [P, 512], F32)) for b in range(2)]
        psC = [ctx.enter_context(nc.psum_tensor(f"psC{b}", [P, 512], F32)) for b in range(2)]
        psR = [ctx.enter_context(nc.psum_tensor(f"psR{b}", [P, 512], F32)) for b in range(2)]

        YR = 2 * T + 2 * P
        table = nc.dram_tensor("table", [T, XGW], F32)
        planes = [nc.dram_tensor(f"plane{c}", [YR, D], F32) for c in range(CHAINS)]

        x_loaded = [sem(f"x_loaded{g}") for g in range(NC)]
        const_loaded = sem("const_loaded")
        raw_loaded = sem("raw_loaded")
        late_loaded = sem("late_loaded")
        diag_made = sem("diag_made")
        hi_made = sem("hi_made")
        lo_made = sem("lo_made")
        xf_ready = sem("xf_ready")
        xhi_ready = sem("xhi_ready")
        shared_added = sem("shared_added")
        w_hi = sem("w_hi")
        w_split = sem("w_split")
        w_loaded = [sem(f"w_loaded{b}") for b in range(WR)]
        T_full = [sem(f"T_full{b}") for b in range(2)]
        T_free = [sem(f"T_free{b}") for b in range(2)]
        A_full = [sem(f"A_full{b}") for b in range(2)]
        A_free = [sem(f"A_free{b}") for b in range(2)]
        C_full = [sem(f"C_full{b}") for b in range(2)]
        C_free = [sem(f"C_free{b}") for b in range(2)]
        dve_step = sem("dve_step")
        act_step = sem("act_step")
        mean_var = sem("mean_var")
        rstd_ready = sem("rstd_ready")
        root_step = sem("root_step")
        planes_paired = sem("planes_paired")
        cum_ready = sem("cum_ready")
        xn_ready = sem("xn_ready")
        xt_ready = sem("xt_ready")
        xn_stored = sem("xn_stored")
        gates_ready = sem("gates_ready")
        gates_stored = sem("gates_stored")
        logits_ready = sem("logits_ready")
        scores_ready = sem("scores_ready")
        mask_ready = sem("mask_ready")
        maskT_ready = sem("maskT_ready")
        list_split = sem("list_split")
        list_joined = sem("list_joined")
        slots_ready = sem("slots_ready")
        keyslot_ready = sem("keyslot_ready")
        idx_ready = sem("idx_ready")
        hid_ready = sem("hid_ready")
        shared_ready = sem("shared_ready")
        planes_zero = [sem(f"planes_zero{c}") for c in range(CHAINS)]
        const_made = sem("const_made")
        gathered = [sem(f"gathered{b}") for b in range(XR)]
        xd_ready = sem("xd_ready")
        gc_ready = sem("gc_ready")
        relu_ready = sem("relu_ready")
        h_ready = sem("h_ready")
        yo_ready = sem("yo_ready")
        scattered = [sem(f"scattered{c}") for c in range(CHAINS)]
        plane_loaded = [sem(f"plane_loaded{b}") for b in range(2)]
        plane_used = sem("plane_used")
        hA_ready = sem("hA_ready")
        gT_ready = sem("gT_ready")
        uv_used = sem("uv_used")
        go_ready = sem("go_ready")
        att_out = sem("att_out")
        x_final = sem("x_final")
        out_stored = sem("out_stored")

        NPAIR = NT // 2
        T_ln = [0, NPAIR + NP, 2 * NPAIR + NP]
        T_ex = [NPAIR, 3 * NPAIR + NP]
        UP = NC * HB
        NA = 3 + 2 * KD * 2 - 2 + 0
        ATT_A = 1 + 3 * KD
        A_up = [0, UP + NP + NC * ATT_A]
        A_ex = [UP, 2 * UP + NP + NC * ATT_A]
        A_att = UP + NP
        C_dn = [0, NPAIR + NP + NPAIR]
        C_ex = [NPAIR, 3 * NPAIR + NP]
        C_att = NPAIR + NP

        def full(sems, n):
            return sems[n % 2], n // 2 + 1

        def scatters(f, i, c):
            return f * len(range(c, NP, CHAINS)) + len(range(c, i, CHAINS))

        x_t = x.rearrange("(t p) d -> p t d", p=P)
        out_t = out.rearrange("(t p) d -> p t d", p=P)
        table_t = table[:, :].rearrange("(t p) w -> p t w", p=P)
        plane_t = [pl[0:2 * T, :].rearrange("(t p c) d -> p t (c d)", p=P, c=2) for pl in planes]

        block = ctx.enter_context(nc.Block())

        @block.sync
        def _(sp):
            sp.dma_start(X[:, 0:TC, :], x_t[:, 0:TC, :]).then_inc(x_loaded[0], 16)
            sp.dma_start(cst[:, :], consts).then_inc(const_loaded, 16)
            sp.dma_start(vec[:, :], vecs).then_inc(const_loaded, 16)
            sp.dma_start(X[:, TC:2 * TC, :], x_t[:, TC:2 * TC, :]).then_inc(x_loaded[1], 16)
            sp.dma_start(raw[:, 0:wsplit.shape[1]], wsplit).then_inc(raw_loaded, 16)
            sp.dma_start(cbs[:, :], convb).then_inc(raw_loaded, 16)
            for g in range(2, NC):
                sp.dma_start(X[:, g * TC:(g + 1) * TC, :], x_t[:, g * TC:(g + 1) * TC, :]).then_inc(x_loaded[g], 16)
            for dst, src in ((eb[:, :], ebias), (sd[:, :, :], sdown), (keyrow[:, :], keys), (wus[:, :, :], wu),
                             (wg2s[:, :], wg2)):
                sp.dma_start(dst, src).then_inc(late_loaded, 16)

            def clear_planes(g):
                rows = YR // P
                a, b = g * rows // NC, (g + 1) * rows // NC
                for c in range(CHAINS):
                    dst = planes[c][:, :].rearrange("(p r) d -> p r d", p=P)[:, a:b, :]
                    sp.dma_start(dst, zero[:, None, :].to_broadcast([P, b - a, D])).then_inc(planes_zero[c], 16)

            def load_weights(f, i):
                n = f * NP + i
                if n >= WR:
                    b, a = divmod(n - WR, NP)
                    sp.wait_ge(*full(C_full, C_ex[b] + a))
                    sp.wait_ge(w_split, n - WR + 1)
                sp.dma_start(W[:, n % WR, :, :], wexp[:, 2 * i:2 * i + 2, :]).then_inc(w_loaded[n % WR], 16)

            for f in range(2):
                if f == 0:
                    sp.wait_ge(const_made, 1)
                for g in range(NC):
                    if f == 0:
                        clear_planes(g)
                    sp.wait_ge(xn_ready, (2 * f * NC) + g + 1)
                    sp.dma_start(table_t[:, g * TC:(g + 1) * TC, 0:D],
                                 XN[:, g * TC:(g + 1) * TC, :, :].rearrange("p t h d -> p t (h d)").bitcast(F32)
                                 ).then_inc(xn_stored, 16)
                for q in range(WR):
                    load_weights(f, q)
                sp.wait_ge(gates_ready, NC * (f + 1))
                sp.dma_start(table_t[:, :, D:XGW], gates[:, :, :]).then_inc(gates_stored, 16)
                sp.wait_ge(list_split, f + 1)
                sp.dma_start(lst[0:CAP, CAP:P], lst[CAP:P, 0:CAP]).then_inc(list_joined, 16)
                for q in range(WR, NP):
                    load_weights(f, q)
                for g in range(NC):
                    n = f * NC + g
                    b = n % 2
                    for c in range(CHAINS):
                        sp.wait_ge(scattered[c], 16 * scatters(f, NP, c))
                    if g >= 2:
                        sp.wait_ge(plane_used, n - 1)
                    elif f == 0:
                        pass
                    for c in range(CHAINS):
                        sp.dma_start(PL[:, b, :, 2 * c:2 * c + 2, :],
                                     plane_t[c][:, g * TC:(g + 1) * TC, :].rearrange("p t (c d) -> p t c d", c=2)
                                     ).then_inc(plane_loaded[b], 16)
                if f == 0:
                    for b in range(2):
                        sp.wait_ge(plane_loaded[b], 16 * CHAINS * (NC // 2))
                    for g in range(NC):
                        clear_planes(g)
            for g in range(NC):
                sp.wait_ge(x_final, g + 1)
                sp.dma_start(out_t[:, g * TC:(g + 1) * TC, :], X[:, g * TC:(g + 1) * TC, :]).then_inc(out_stored, 16)
            sp.wait_ge(out_stored, 16 * NC)

        @block.gpsimd
        def _(pool):
            pool.memset(zero[:, :], 0.0).then_inc(const_made, 1)
            pool.memset(mh[:, :], -0.5)
            pool.memset(one16[:, :], 1.0)
            for a in (0, 1):
                pool.memset(XT[:, :, :, a:a + T // L * SW + 1:SW], 0.0)
            pool.memset(XG[:, :, :], 0.0).then_inc(const_made, 1)
            pool.wait_ge(const_made, 2)

            def roots(ln, g):
                pool.wait_ge(mean_var, ln * NC + g + 1)
                gs = slice(g * TC, (g + 1) * TC)
                pool.tensor_tensor(rstd[:, gs], mv[:, gs, 1], mh[:, :], ALU.pow).then_inc(root_step, 1)
                pool.wait_ge(root_step, ln * NC + g + 1)
                pool.tensor_tensor(shift[:, gs], negmean[:, gs], rstd[:, gs], ALU.mult).then_inc(rstd_ready, 1)

            def low_half(ln, g):
                pool.wait_ge(xhi_ready, ln * NC + g + 1)
                pool.tensor_tensor(XN[:, g * TC:(g + 1) * TC, 1, :], XF[:, :, :], XN[:, g * TC:(g + 1) * TC, 0, :],
                                   ALU.subtract).then_inc(xn_ready, 1)

            for g in range(NC + 1):
                if g < NC:
                    roots(0, g)
                if g == 1:
                    pool.wait_ge(hi_made, 2)
                    pool.tensor_tensor(cb16[:, 1, :], cbs[:, :], cb16[:, 0, :], ALU.subtract)
                    pool.tensor_tensor(w16[:, 1, 0:KD * E], raw[:, 0:KD * E], w16[:, 0, 0:KD * E],
                                       ALU.subtract).then_inc(lo_made, 1)
                if g >= 1:
                    low_half(0, g - 1)
            pool.tensor_tensor(w16[:, 1, KD * E:], raw[:, KD * E:], w16[:, 0, KD * E:],
                               ALU.subtract).then_inc(lo_made, 1)
            for f in range(2):
                for q in range(NPAIR):
                    n = f * NPAIR + q
                    pool.wait_ge(shared_ready, n + 1)
                    xs = X[:, 2 * q:2 * q + 2, :].rearrange("p t d -> p (t d)")
                    pool.tensor_tensor(xs, xs, S[:, n % 2, :], ALU.add).then_inc(shared_added, 1)
                pool.wait_ge(idx_ready, f + 1)
                pool.wait_ge(xn_stored, 16 * NC * (f + 1))
                pool.wait_ge(gates_stored, 16 * (f + 1))

                def gather(i):
                    n = f * NP + i
                    if n >= XR:
                        pool.wait_ge(*full(T_full, T_ex[f] + i - XR if i >= XR else T_ex[0] + NP - XR + i))
                        pool.wait_ge(gc_ready, n - XR + 1)
                    pool.indirect_dma_start(XG[:, n % XR, :], None, table[:, :],
                                            bass.IndirectOffsetOnAxis(ap=gidx[:, i:i + 1], axis=0),
                                            bounds_check=T - 1, oob_is_err=False).then_inc(gathered[n % XR], 16)

                for i in range(XR):
                    gather(i)
                for c in range(CHAINS):
                    pool.wait_ge(planes_zero[c], 16 * NC * (f + 1))
                for i in range(NP):
                    n = f * NP + i
                    pool.wait_ge(yo_ready, n + 1)
                    c = i % CHAINS
                    m = scatters(f, i, c)
                    if m:
                        pool.wait_ge(scattered[c], 16 * m)
                    pool.indirect_dma_start(planes[c][:, :], bass.IndirectOffsetOnAxis(ap=sidx[:, i:i + 1], axis=0),
                                            YO[:, n % 4, :], None, bounds_check=YR - 1, oob_is_err=True,
                                            compute_op=ALU.add).then_inc(scattered[c], 16)
                    if i + XR < NP:
                        gather(i + XR)
                def pair_planes(g):
                    m = f * NC + g
                    pool.wait_ge(plane_loaded[m % 2], 16 * CHAINS * (m // 2 + 1))
                    pool.tensor_tensor(PL[:, m % 2, :, 2, :], PL[:, m % 2, :, 2, :], PL[:, m % 2, :, 3, :],
                                       ALU.add).then_inc(planes_paired, 1)

                if f == 0:
                    for g in range(NC + 1):
                        if g < NC:
                            pair_planes(g)
                        if g >= 1:
                            low_half(1, g - 1)
                        if g < NC:
                            roots(1, g)
                    for c in range(NC + 2):
                        if c < NC:
                            pool.wait_ge(cum_ready, c + 1)
                            if c >= 2:
                                pool.wait_ge(*full(C_full, C_att + (c - 1) * TC // 2 - 1))
                            pool.tensor_tensor(go[:, c % 2, :, :], cum[:, :, :], vg[:, :, :], ALU.mult
                                               ).then_inc(go_ready, 1)
                        if c >= 2:
                            low_half(2, c - 2)
                        if 1 <= c <= NC:
                            roots(2, c - 1)
                else:
                    for g in range(NC):
                        pair_planes(g)

        @block.tensor
        def _(pe):
            def products(out, lhsT, rhs, ks, first=True, last=True):
                todo = [(a, b, k) for a, b in PASSES for k in range(ks)]
                for i, (a, b, k) in enumerate(todo):
                    mm = pe.matmul(out, lhsT(a, k), rhs(b, k), start=first and i == 0, stop=last and i == len(todo) - 1)
                return mm

            def layernorm_T(ln, g):
                pe.wait_ge(xn_ready, ln * NC + g + 1)
                for q in range(g * TC // 2, (g + 1) * TC // 2):
                    n = T_ln[ln] + q
                    if n >= 2:
                        pe.wait_ge(T_free[n % 2], n // 2)
                    pt = psT[n % 2][:, :].bitcast(F16)
                    for h in range(2):
                        for k in range(KD):
                            for j in range(2):
                                b = ((h * KD + k) * 2 + j) * P
                                mm = pe.transpose(pt[:, b:b + P], XN[:, 2 * q + j, h, k * P:(k + 1) * P], ident16[:, :])
                    mm.then_inc(T_full[n % 2], 1)

            def logits(f, g):
                for q in range(g * TC // 2, (g + 1) * TC // 2):
                    pe.wait_ge(xt_ready, 2 * f * NPAIR + q + 1)
                    for j in (2 * q, 2 * q + 1):
                        o = (j // (2 * TC) * TC + j % TC) * E
                        mm = products(psR[g % 2][:, o:o + E], lambda h, k: tokens(h, k, j * P, P),
                                      lambda h, k: gw[:, h, k, :], KD)
                    mm.then_inc(logits_ready, 1)

            def up(f, c):
                for h in range(HB):
                    n = A_up[f] + c * HB + h
                    if n >= 2:
                        pe.wait_ge(A_free[n % 2], n // 2)
                    products(psA[n % 2][:, :], lambda a, k: su[:, a, k, h * P:(h + 1) * P],
                             lambda b, k: tokens(b, k, c * CH, CH), KD).then_inc(A_full[n % 2], 1)

            def down(f, c):
                pe.wait_ge(hid_ready, f * UP + (c + 1) * HB)
                for q in range(TC // 2):
                    n = C_dn[f] + c * TC // 2 + q
                    if n >= 2:
                        pe.wait_ge(C_free[n % 2], n // 2)
                    for j in range(2):
                        tt = (2 * q + j) * P
                        for h in range(HB):
                            mm = pe.matmul(psC[n % 2][:, j * D:(j + 1) * D], HID[:, c % 2, h, tt:tt + P], sd[:, h, :],
                                           start=(h == 0), stop=(h == HB - 1))
                    mm.then_inc(C_full[n % 2], 1)

            def mask_T(f):
                pe.wait_ge(mask_ready, NC * (f + 1))
                pb = psR[0][:, :].bitcast(BF16)
                for t in range(NT // 2):
                    mm = pe.transpose(pb[:, t * P:(t + 1) * P], maskb[:, t, :, :].rearrange("p h e -> p (h e)"), identb[:, :])
                mm.then_inc(maskT_ready, 1)

            def key_slots(f):
                pe.wait_ge(slots_ready, f + 1)
                for h in range(2):
                    mm = pe.matmul(psR[1][h * CAP:(h + 1) * CAP, 0:NP], lstB[0:E, 0:CAP], sel[0:E, h * NP:(h + 1) * NP],
                                   start=True, stop=True)
                mm.then_inc(keyslot_ready, 1)

            def turn(f, i):
                n = f * NP + i
                pe.wait_ge(gathered[n % XR], 16 * (n // XR + 1))
                u = T_ex[f] + i
                pe.wait_ge(T_free[u % 2], u // 2)
                pt, rows = psT[u % 2][:, :].bitcast(F16), XG[:, n % XR, 0:D].bitcast(F16)
                for b in range(2 * KD):
                    mm = pe.transpose(pt[:, b * P:(b + 1) * P], rows[:, b * P:(b + 1) * P], ident16[:, :])
                mm.then_inc(T_full[u % 2], 1)

            def first(f, i):
                n = f * NP + i
                pe.wait_ge(w_split, n + 1)
                pe.wait_ge(xd_ready, n + 1)
                u = A_ex[f] + i
                pe.wait_ge(A_free[u % 2], u // 2)
                for s in range(2):
                    mm = products(psA[u % 2][:, s * CAP:(s + 1) * CAP],
                                  lambda a, k: W1[:, n % SR, a, s, k * I:(k + 1) * I],
                                  lambda b, k: XD[:, n % 3, (b * KD + k) * P + s * CAP:(b * KD + k) * P + (s + 1) * CAP], KD)
                mm.then_inc(A_full[u % 2], 1)

            def second(f, i):
                n = f * NP + i
                pe.wait_ge(h_ready, n + 1)
                u = C_ex[f] + i
                pe.wait_ge(C_free[u % 2], u // 2)
                for s in range(2):
                    mm = pe.matmul(psC[u % 2][s * CAP:(s + 1) * CAP, 0:D], HT2[:, n % 3, s * CAP:(s + 1) * CAP],
                                   W[:, n % WR, s, KD * I:], start=True, stop=True)
                mm.then_inc(C_full[u % 2], 1)
            def ffn(f):
                up(f, 0)
                up(f, 1)
                mask_T(f)
                down(f, 0)
                up(f, 2)
                down(f, 1)
                up(f, 3)
                down(f, 2)
                key_slots(f)
                down(f, 3)
                for s in range(NP + 3):
                    if s < NP:
                        turn(f, s)
                    if 1 <= s <= NP:
                        first(f, s - 1)
                    if s >= 3:
                        second(f, s - 3)

            def attention(c):
                n = [A_att + c * ATT_A]

                def slot():
                    u = n[0]
                    n[0] += 1
                    pe.wait_ge(A_free[u % 2], u // 2)
                    return u
                pe.wait_ge(xt_ready, NPAIR + (c + 1) * TC // 2)
                u = slot()
                products(psA[u % 2][0:DH, :], lambda a, k: wg16[:, a, k, :], lambda b, k: tokens(b, k, c * CH, CH),
                         KD).then_inc(A_full[u % 2], 1)
                pe.wait_ge(hA_ready, c + 1)
                for r in range(KD):
                    u = slot()
                    pe.matmul(psA[u % 2][:, :], wg2s[:, r * P:(r + 1) * P], hA[0:DH, :],
                              start=True, stop=True).then_inc(A_full[u % 2], 1)
                for w in (wu16, wv16):
                    for r in range(KD):
                        u = slot()
                        products(psA[u % 2][:, :], lambda a, k: w[:, a, k, r * P:(r + 1) * P],
                                 lambda b, k: tokens(b, k, c * CH, CH), KD).then_inc(A_full[u % 2], 1)

            def att_project(c):
                pe.wait_ge(go_ready, c + 1)
                for q in range(TC // 2):
                    u = C_att + c * TC // 2 + q
                    pe.wait_ge(C_free[u % 2], u // 2)
                    for j in range(2):
                        tt = (2 * q + j) * P
                        for h in range(2):
                            pe.matmul(psC[u % 2][:, j * D:(j + 1) * D], one16[:, :], cb16[:, h, :],
                                      start=(h == 0), stop=False)
                        for k in range(KD):
                            for tap in range(3):
                                products(psC[u % 2][:, j * D + k * P:j * D + (k + 1) * P],
                                         lambda a, _: tokens(a, k, c * CH + tt, P, tap - 1),
                                         lambda b, _: diag[:, b, tap, k, :], 1, False, False)
                        for r in range(KD):
                            mm = pe.matmul(psC[u % 2][:, j * D:(j + 1) * D], go[:, c % 2, r, tt:tt + P],
                                           wus[:, r, :], start=False, stop=(r == KD - 1))
                    mm.then_inc(C_full[u % 2], 1)

            pe.wait_ge(dve_step, 2)
            for g in range(NC):
                layernorm_T(0, g)
                if g == 0:
                    pe.wait_ge(lo_made, 1)
                logits(0, g)
            pe.wait_ge(lo_made, 2)
            pe.wait_ge(late_loaded, 16 * 5)
            ffn(0)
            for g in range(NC):
                layernorm_T(1, g)
            for c in range(NC + 2):
                if c < NC:
                    attention(c)
                if 1 <= c <= NC:
                    att_project(c - 1)
                if c >= 2:
                    layernorm_T(2, c - 2)
                    logits(1, c - 2)
            ffn(1)

        @block.scalar
        def _(act):
            steps = [0]

            def link(ins):
                steps[0] += 1
                ins.then_inc(act_step, 1)
                act.wait_ge(act_step, steps[0])

            def normal(ln, g):
                act.wait_ge(rstd_ready, ln * NC + g + 1)
                if ln * NC + g:
                    act.wait_ge(xn_ready, ln * NC + g)
                if ln:
                    act.wait_ge(*full(T_full, T_ln[ln - 1] + (g + 1) * TC // 2 - 1))
                    if ln == 1:
                        act.wait_ge(xn_stored, 16 * NC)
                for j in range(TC):
                    t = g * TC + j
                    ins = act.activation(XF[:, j, :], X[:, t, :], ACT.Identity, bias=shift[:, t:t + 1],
                                         scale=rstd[:, t:t + 1])
                ins.then_inc(xf_ready, 1)
                act.wait_ge(xf_ready, ln * NC + g + 1)
                act.activation(XN[:, g * TC:(g + 1) * TC, 0, :], XF[:, :, :], ACT.Copy).then_inc(xhi_ready, 1)

            def scores(f, g):
                act.wait_ge(logits_ready, f * NPAIR + (g + 1) * TC // 2)
                if f * NC + g:
                    act.wait_ge(gates_ready, f * NC + g)
                o = g // 2 * TC * E
                act.activation(sco[:, :, :], psR[g % 2][:, o:o + TC * E].rearrange("p (t e) -> p t e", e=E),
                               ACT.Sigmoid).then_inc(scores_ready, 1)

            def xt_copy(ln, g):
                for q in range(g * TC // 2, (g + 1) * TC // 2):
                    n = T_ln[ln] + q
                    act.wait_ge(*full(T_full, n))
                    act.copy(XT[:, :, :, q * SW + 2:(q + 1) * SW].rearrange("p h k l -> p (h k) l").bitcast(F32),
                             psT[n % 2][:, :].rearrange("p (a t) -> p a t", a=2 * KD)).then_inc(xt_ready, 1)
                    act.wait_ge(xt_ready, ln * NPAIR + q + 1)
                    act.nop().then_inc(T_free[n % 2], 1)

            def hidden(f, c):
                for h in range(HB):
                    n = A_up[f] + c * HB + h
                    act.wait_ge(*full(A_full, n))
                    if h == 0 and f * NC + c >= 2:
                        pass
                    link(act.activation(HID[:, c % 2, h, :], psA[n % 2][:, :], ACT.Relu))
                    act.nop().then_inc(A_free[n % 2], 1)
                    act.activation(HID[:, c % 2, h, :], HID[:, c % 2, h, :], ACT.Square).then_inc(hid_ready, 1)

            def shared_out(f, c):
                for q in range(TC // 2):
                    n = C_dn[f] + c * TC // 2 + q
                    act.wait_ge(*full(C_full, n))
                    z = f * NPAIR + c * TC // 2 + q
                    if z >= 2:
                        act.wait_ge(shared_added, z - 1)
                    act.activation(S[:, z % 2, :], psC[n % 2][:, :], ACT.Copy, scale=HALF).then_inc(shared_ready, 1)
                    act.wait_ge(shared_ready, z + 1)
                    act.nop().then_inc(C_free[n % 2], 1)

            def ffn(f):
                hidden(f, 0)
                hidden(f, 1)
                shared_out(f, 0)
                hidden(f, 2)
                shared_out(f, 1)
                hidden(f, 3)
                shared_out(f, 2)
                shared_out(f, 3)

                def relu(i):
                    n = f * NP + i
                    u = A_ex[f] + i
                    act.wait_ge(*full(A_full, u))
                    if n >= 3:
                        act.wait_ge(h_ready, n - 2)
                    act.activation(RH[:, n % 3, :], psA[u % 2][:, 0:P], ACT.Relu).then_inc(relu_ready, 1)
                    act.wait_ge(relu_ready, n + 1)
                    act.nop().then_inc(A_free[u % 2], 1)

                def gated(i):
                    n = f * NP + i
                    u = C_ex[f] + i
                    act.wait_ge(*full(C_full, u))
                    act.wait_ge(gc_ready, n + 1)
                    if n >= 4:
                        b, a = divmod(n - 4, NP)
                        act.wait_ge(scattered[a % CHAINS], 16 * (scatters(b, a, a % CHAINS) + 1))
                    act.activation(YO[:, n % 4, :], psC[u % 2][:, 0:D], ACT.Copy, scale=GC[:, n % 4:n % 4 + 1]
                                   ).then_inc(yo_ready, 1)
                    act.wait_ge(yo_ready, n + 1)
                    act.nop().then_inc(C_free[u % 2], 1)

                def weights_hi(i):
                    m = f * NP + i
                    act.wait_ge(w_loaded[m % WR], 16 * (m // WR + 1))
                    if m >= SR:
                        b, a = divmod(m - SR, NP)
                        act.wait_ge(*full(A_full, A_ex[b] + a))
                    act.activation(W1[:, m % SR, 0, :, :], W[:, m % WR, :, 0:KD * I], ACT.Copy).then_inc(w_hi, 1)

                weights_hi(0)
                weights_hi(1)
                for s in range(NP + 3):
                    if 1 <= s <= NP:
                        relu(s - 1)
                    if s >= 3:
                        gated(s - 3)
                    if s + 2 < NP:
                        weights_hi(s + 2)

            def attention(c):
                n = A_att + c * ATT_A
                act.wait_ge(*full(A_full, n))
                act.activation(hA[0:DH, :], psA[n % 2][0:DH, :], ACT.Relu, bias=bg1).then_inc(hA_ready, 1)
                act.wait_ge(hA_ready, c + 1)
                act.nop().then_inc(A_free[n % 2], 1)
                if c >= 1:
                    act.wait_ge(uv_used, 4 * c)
                for r in range(KD):
                    u = n + 1 + r
                    act.wait_ge(*full(A_full, u))
                    act.activation(gT[:, r, :], psA[u % 2][:, :], ACT.Sigmoid, bias=bg2[:, r:r + 1]).then_inc(gT_ready, 1)
                    act.wait_ge(gT_ready, c * KD + r + 1)
                    act.nop().then_inc(A_free[u % 2], 1)

            for g in range(NC + 1):
                if g < NC:
                    normal(0, g)
                if g == 0:
                    act.wait_ge(raw_loaded, 32)
                    act.wait_ge(diag_made, 1)
                    act.activation(w16[:, 0, :], raw, ACT.Copy).then_inc(hi_made, 1)
                    act.activation(cb16[:, 0, :], cbs[:, :], ACT.Copy).then_inc(hi_made, 1)
                    act.wait_ge(const_made, 2)
                if g:
                    xt_copy(0, g - 1)
                    scores(0, g - 1)
            act.wait_ge(const_loaded, 32)
            act.wait_ge(lo_made, 2)
            ffn(0)
            for g in range(NC + 1):
                if g < NC:
                    normal(1, g)
                if g:
                    xt_copy(1, g - 1)
            for c in range(NC + 2):
                if c < NC:
                    attention(c)
                if c >= 2:
                    normal(2, c - 2)
                    xt_copy(2, c - 2)
                    scores(1, c - 2)
            ffn(1)

        @block.vector
        def _(dve):
            steps = [0]

            def link(ins):
                steps[0] += 1
                ins.then_inc(dve_step, 1)
                dve.wait_ge(dve_step, steps[0])

            def stats(ln, g):
                for j in range(g * TC, (g + 1) * TC):
                    ins = dve.bn_stats(st[:, j, :], X[:, j, :])
                link(ins)
                for j in range(g * TC, (g + 1) * TC):
                    ins = dve.bn_aggr(mv[:, j, :], st[:, j, :])
                link(ins)
                gs = slice(g * TC, (g + 1) * TC)
                dve.tensor_scalar(negmean[:, gs], mv[:, gs, 0], -1.0, None, ALU.mult)
                dve.tensor_scalar(mv[:, gs, 1], mv[:, gs, 1], EPS, None, ALU.add).then_inc(mean_var, 1)

            dve.wait_ge(const_loaded, 32)
            link(dve.tensor_copy(identb[:, :], ident))
            link(dve.tensor_copy(ident16[:, :], ident))
            for j in range(3):
                for k in range(KD):
                    b = wsplit.shape[1] + (j * KD + k) * P
                    ins = dve.tensor_scalar(raw[:, b:b + P], ident, cw[j][:, k:k + 1], None, ALU.mult)
            ins.then_inc(diag_made, 1)

            def route(f, g):
                n = f * NC + g
                gs = slice(g * TC, (g + 1) * TC)
                dve.wait_ge(scores_ready, n + 1)
                if n == 0:
                    dve.wait_ge(late_loaded, 16 * 5)
                link(dve.memset(msk[:, :, E:E + 2], 2 * FAR))
                link(dve.tensor_tensor(scb[:, :, :], sco[:, :, :], eb[:, None, :].to_broadcast([P, TC, E]), ALU.add))
                a = scb[:, :, :].rearrange("p t (g s) -> p (t g) s", s=GS)
                NG = TC * NGRP
                q = NG * 4
                hi = tA[:, 0:q].rearrange("p (g s) -> p g s", s=4)
                lo = tA[:, q:2 * q].rearrange("p (g s) -> p g s", s=4)
                dve.tensor_tensor(hi, a[:, :, 0:4], a[:, :, 4:8], ALU.max)
                link(dve.tensor_tensor(lo, a[:, :, 0:4], a[:, :, 4:8], ALU.min))
                q = NG * 2
                h2 = tB[:, 0:q].rearrange("p (g s) -> p g s", s=2)
                m2 = tB[:, q:2 * q].rearrange("p (g s) -> p g s", s=2)
                l2 = tC[:, 0:q].rearrange("p (g s) -> p g s", s=2)
                n2 = tC[:, q:2 * q].rearrange("p (g s) -> p g s", s=2)
                dve.tensor_tensor(h2, hi[:, :, 0:2], hi[:, :, 2:4], ALU.max)
                dve.tensor_tensor(m2, hi[:, :, 0:2], hi[:, :, 2:4], ALU.min)
                link(dve.tensor_tensor(l2, lo[:, :, 0:2], lo[:, :, 2:4], ALU.max))
                link(dve.tensor_tensor(n2, m2, l2, ALU.max))
                h1, m1, l1, n1 = (tA[:, NG * z:NG * (z + 1)] for z in range(4))
                dve.tensor_tensor(h1, h2[:, :, 0], h2[:, :, 1], ALU.max)
                dve.tensor_tensor(m1, h2[:, :, 0], h2[:, :, 1], ALU.min)
                link(dve.tensor_tensor(l1, n2[:, :, 0], n2[:, :, 1], ALU.max))
                link(dve.tensor_tensor(n1, m1, l1, ALU.max))
                link(dve.tensor_tensor(gsc[:, :, :].rearrange("p t g -> p (t g)"), h1, n1, ALU.add))
                B = [P, TC, NGRP, NGRP]
                other = gsc[:, :, None, :].to_broadcast(B)
                mine = gsc[:, :, :, None].to_broadcast(B)
                g4 = lambda z: z.rearrange("p (t g s) -> p t g s", g=NGRP, s=NGRP)
                low = lower.rearrange("p (g s) -> p g s", s=NGRP)
                dve.tensor_tensor(g4(tA), other, mine, ALU.is_gt)
                link(dve.tensor_tensor(g4(tB), other, mine, ALU.is_equal))
                link(dve.tensor_tensor(g4(tB), g4(tB), low[:, None, :, :].to_broadcast(B), ALU.mult))
                link(dve.tensor_tensor(tA, tA, tB, ALU.add))
                link(dve.tensor_reduce(gpen[:, :, :], g4(tA), AX.X, ALU.add))
                link(dve.tensor_scalar(gpen[:, :, :], gpen[:, :, :], TOPG - 0.5, -FAR, ALU.is_gt, ALU.mult))
                link(dve.tensor_tensor(msk[:, :, 0:E].rearrange("p t (g s) -> p t g s", s=GS),
                                       scb[:, :, :].rearrange("p t (g s) -> p t g s", s=GS),
                                       gpen[:, :, :, None].to_broadcast([P, TC, NGRP, GS]), ALU.add))
                for t in range(TC):
                    ins = dve.max(top[:, t, :], msk[:, t, 0:E])
                link(ins)
                link(dve.memset(top[:, :, TOPK:8], 2 * FAR))
                for t in range(TC):
                    ins = dve.match_replace(rept[:, t, :], top[:, t, :], msk[:, t, :], FAR)
                link(ins)
                if f and g == 0:
                    dve.wait_ge(maskT_ready, 1)
                q = g % 2 * TC
                dve.tensor_scalar(maskb[:, q:q + TC, g // 2, :], rept[:, :, 0:E], FAR, None, ALU.is_equal
                                  ).then_inc(mask_ready, 1)
                t3 = lambda z: z.rearrange("p (t e) -> p t e", e=E)
                link(dve.tensor_scalar(t3(tA), rept[:, :, 0:E], FAR, None, ALU.is_equal))
                link(dve.tensor_tensor(tC, tA, sco[:, :, :].rearrange("p t e -> p (t e)"), ALU.mult))
                link(dve.tensor_reduce(wsum, t3(tC), AX.X, ALU.add))
                link(dve.tensor_scalar(wsum, wsum, 1e-20, None, ALU.add))
                link(dve.reciprocal(wrec, wsum))
                link(dve.tensor_scalar(wrec, wrec, ROUTE_SCALE * HALF, None, ALU.mult))
                if f and g == 0:
                    dve.wait_ge(gates_stored, 16)
                dve.tensor_tensor(gates[:, gs, :], t3(tC), wrec[:, :, None].to_broadcast([P, TC, E]), ALU.mult
                                  ).then_inc(gates_ready, 1)

            def search(f):
                dve.wait_ge(maskT_ready, f + 1)
                link(dve.tensor_tensor(keyA, psR[0][:, :].bitcast(BF16), keyrow[:, :], ALU.mult))
                a, b = keyA, keyB
                for r in range(CAP // 8):
                    link(dve.max(lst[:, r * 8:(r + 1) * 8], a))
                    if r < CAP // 8 - 1:
                        link(dve.match_replace(b, lst[:, r * 8:(r + 1) * 8], a, 0.0))
                        a, b = b, a
                dve.nop().then_inc(list_split, 1)
                dve.wait_ge(list_joined, 16 * (f + 1))
                a, b = lst, lstA
                for r in range(CAP // 8):
                    link(dve.max(lstB[0:CAP, r * 8:(r + 1) * 8], a[0:CAP, :]))
                    if r < CAP // 8 - 1:
                        link(dve.match_replace(b[0:CAP, :], lstB[0:CAP, r * 8:(r + 1) * 8], a[0:CAP, :], 0.0))
                        a, b = b, a
                dve.nop().then_inc(slots_ready, 1)
                dve.wait_ge(keyslot_ready, f + 1)
                tok, emp = slot_a, slot_b
                key = psR[1][:, 0:NP]
                dve.tensor_scalar(gidx[:, :], key, -1.0, float(T), ALU.mult, ALU.add)
                dve.tensor_scalar(tok, key, -2.0, 2.0 * T, ALU.mult, ALU.add)
                link(dve.tensor_scalar(emp, key, 0.0, slotno, ALU.is_equal, ALU.mult))
                link(dve.tensor_tensor(tok, tok, emp, ALU.add))
                link(dve.tensor_scalar(sidx[:, :], tok, half, None, ALU.add))
                dve.nop().then_inc(idx_ready, 1)

            def experts(f):
                def xd(i):
                    n = f * NP + i
                    u = T_ex[f] + i
                    dve.wait_ge(*full(T_full, u))
                    if n >= 3:
                        m = A_ex[f] + i - 3 if i >= 3 else A_ex[0] + NP - 3 + i
                        dve.wait_ge(*full(A_full, m))
                    dve.tensor_copy(XD[:, n % 3, :].bitcast(F32), psT[u % 2][:, 0:KD * P]).then_inc(xd_ready, 1)
                    if n >= 4:
                        dve.wait_ge(yo_ready, n - 3)
                    dve.tensor_tensor_reduce(out=GJ[:, n % 4, :], in0=XG[:, n % XR, D + 2 * i:D + 2 * i + 2], in1=parity,
                                             scale=1.0, scalar=0.0, op0=ALU.mult, op1=ALU.add,
                                             accum_out=GC[:, n % 4:n % 4 + 1]).then_inc(gc_ready, 1)
                    dve.wait_ge(xd_ready, n + 1)
                    dve.nop().then_inc(T_free[u % 2], 1)

                def square(i):
                    n = f * NP + i
                    dve.wait_ge(relu_ready, n + 1)
                    if n >= 3:
                        m = C_ex[f] + i - 3 if i >= 3 else C_ex[0] + NP - 3 + i
                        dve.wait_ge(*full(C_full, m))
                    dve.tensor_tensor(HT2[:, n % 3, :], RH[:, n % 3, :], RH[:, n % 3, :], ALU.mult).then_inc(h_ready, 1)

                def weights_lo(i):
                    m = f * NP + i
                    dve.wait_ge(w_hi, m + 1)
                    dve.tensor_tensor(W1[:, m % SR, 1, :, :], W[:, m % WR, :, 0:KD * I], W1[:, m % SR, 0, :, :],
                                      ALU.subtract).then_inc(w_split, 1)

                weights_lo(0)
                weights_lo(1)
                for s in range(NP + 2):
                    if s < NP:
                        xd(s)
                    if s >= 2:
                        square(s - 2)
                    if s + 2 < NP:
                        weights_lo(s + 2)

            def combine(f, g):
                n = f * NC + g
                b = n % 2
                gs = slice(g * TC, (g + 1) * TC)
                dve.wait_ge(shared_added, f * NPAIR + (g + 1) * TC // 2)
                dve.wait_ge(plane_loaded[b], 16 * CHAINS * (n // 2 + 1))
                for c in range(3):
                    if c == 2:
                        dve.wait_ge(planes_paired, n + 1)
                    ins = dve.tensor_tensor(X[:, gs, :], X[:, gs, :], PL[:, b, :, c, :], ALU.add)
                    if c < 2 or f == 0:
                        link(ins)
                if f:
                    ins.then_inc(x_final, 1)
                    dve.wait_ge(x_final, g + 1)
                dve.nop().then_inc(plane_used, 1)

            def attention(c):
                n = A_att + c * ATT_A
                dve.wait_ge(gT_ready, KD * (c + 1))
                if c:
                    dve.wait_ge(go_ready, c)
                for z, (dst, b) in enumerate(((ug, bu), (vg, bv))):
                    for r in range(KD):
                        u = n + 1 + KD + z * KD + r
                        dve.wait_ge(*full(A_full, u))
                        link(dve.scalar_tensor_tensor(out=dst[:, r, :], in0=psA[u % 2][:, :], scalar=b[:, r:r + 1],
                                                      in1=gT[:, r, :], op0=ALU.add, op1=ALU.mult))
                        dve.nop().then_inc(A_free[u % 2], 1)
                        dve.nop().then_inc(uv_used, 1)
                for r in range(KD):
                    for s in range(SEQ):
                        ins = dve.tensor_tensor_scan(cum[:, r, s * L:(s + 1) * L], ones, ug[:, r, s * L:(s + 1) * L],
                                                     0.0, ALU.mult, ALU.add)
                ins.then_inc(cum_ready, 1)

            def att_residual(c):
                for q in range(TC // 2):
                    u = C_att + c * TC // 2 + q
                    j = c * TC + 2 * q
                    dve.wait_ge(*full(C_full, u))
                    link(dve.tensor_tensor(X[:, j:j + 2, :], X[:, j:j + 2, :],
                                           psC[u % 2][:, :].rearrange("p (t d) -> p t d", d=D), ALU.add))
                    dve.nop().then_inc(C_free[u % 2], 1)

            for g in range(NC):
                dve.wait_ge(x_loaded[g], 16)
                stats(0, g)
            for g in range(NC):
                route(0, g)
            search(0)
            experts(0)
            for g in range(NC):
                combine(0, g)
                stats(1, g)
            for c in range(NC + 3):
                if c < NC:
                    attention(c)
                if c >= 3:
                    route(1, c - 3)
                if 1 <= c <= NC:
                    att_residual(c - 1)
                    stats(2, c - 1)
            search(1)
            experts(1)
            for g in range(NC):
                combine(1, g)


def kernel(L0_attn_x, L0_attn_Wu, L0_attn_bu, L0_attn_Wv, L0_attn_bv, L0_attn_Wg1, L0_attn_bg1, L0_attn_Wg2,
           L0_attn_bg2, L0_attn_conv_w, L0_attn_conv_b, L0_ffn_gate_w, L0_ffn_e_bias, L0_ffn_w1, L0_ffn_w2,
           L0_ffn_shared_up_w, L0_ffn_shared_down_w):
    import numpy as np
    import concourse.bacc as bacc
    from concourse.bass_utils import run_bass_kernel_spmd

    def blocks(w):
        w = np.asarray(w)
        return np.ascontiguousarray(w.reshape(-1, P, w.shape[1]).transpose(1, 0, 2))

    x = np.asarray(L0_attn_x)
    B, L, D = x.shape
    T = B * L
    w1, w2 = np.asarray(L0_ffn_w1), np.asarray(L0_ffn_w2)
    E, I, _ = w1.shape
    KD = D // P
    w1l = w1.transpose(2, 0, 1).reshape(KD, P, E, I).transpose(1, 2, 0, 3).reshape(P, E, KD * I)
    w2l = w2.transpose(2, 0, 1)
    wexp = np.ascontiguousarray(np.concatenate([w1l, w2l], axis=2))
    col = lambda v: np.asarray(v).reshape(KD, P).T
    cw = np.asarray(L0_attn_conv_w)[:, 0, :]
    bg1 = np.asarray(L0_attn_bg1)
    vecs = np.ascontiguousarray(np.concatenate(
        [col(L0_attn_bu), col(L0_attn_bv), col(L0_attn_bg2),
         col(cw[:, 0]), col(cw[:, 1]), col(cw[:, 2]),
         np.pad(bg1, (0, P - bg1.size)).reshape(P, 1)], axis=1))
    p = np.arange(P)
    lower = (np.arange(NGRP)[None, :] < np.arange(NGRP)[:, None]).astype(np.float32)
    NP = E // 2
    sel = np.zeros((P, 2, NP), np.float32)
    for e in range(E):
        sel[e, e % 2, e // 2] = 1
    keyrow = T - (p[:, None] // E * (T // 2) + np.arange(T // 2)[None, :])
    consts = np.ascontiguousarray(np.concatenate(
        [np.eye(P), np.broadcast_to(lower.reshape(1, -1), (P, NGRP * NGRP)), np.ones((P, L)),
         np.stack([p < CAP, p >= CAP], 1), (p >= CAP)[:, None], p[:, None], sel.reshape(P, -1)],
        axis=1).astype(np.float32))
    arrays = {
        "x": np.ascontiguousarray(x.reshape(T, D)), "wexp": wexp,
        "ebias": np.ascontiguousarray(np.broadcast_to(np.asarray(L0_ffn_e_bias)[None, :], (P, E))),
        "wsplit": np.ascontiguousarray(np.concatenate(
            [blocks(np.asarray(w).T).reshape(P, -1) for w in
             (L0_ffn_gate_w, L0_ffn_shared_up_w, L0_attn_Wu, L0_attn_Wv, L0_attn_Wg1)], axis=1)),
        "sdown": blocks(np.asarray(L0_ffn_shared_down_w).T),
        "wu": blocks(np.asarray(L0_attn_Wu).T), "wg2": np.ascontiguousarray(np.asarray(L0_attn_Wg2).T),
        "convb": np.ascontiguousarray(np.asarray(L0_attn_conv_b).reshape(1, D)),
        "vecs": vecs, "consts": consts, "keys": np.ascontiguousarray(keyrow.astype(np.float32)),
    }
    nc = bacc.Bacc("TRN2", target_bir_lowering=False, num_devices=1)
    args = [nc.dram_tensor(n, a.shape, mybir.dt.from_np(a.dtype), kind="ExternalInput").ap() for n, a in arrays.items()]
    out = nc.dram_tensor("out", (T, D), F32, kind="ExternalOutput").ap()
    build(nc, *args, out)
    r = run_bass_kernel_spmd(nc, [arrays], core_ids=[0])
    return r.results[0]["out"].reshape(B, L, D)
```

```python
from contextlib import ExitStack

import concourse.bass as bass
from concourse import mybir

ALU = mybir.AluOpType
ACT = mybir.ActivationFunctionType
AX = mybir.AxisListType
F32 = mybir.dt.float32
BF16 = mybir.dt.bfloat16
F16 = mybir.dt.float16
U32 = mybir.dt.uint32

P = 128
EPS = 1e-5
TOPK = 6
NGRP = 8
TOPG = 4
CAP = 64
ROUTE_SCALE = 2.5
HALF = 0.5
FAR = 1e30


PASSES = ((0, 0), (1, 0), (0, 1))


def build(nc, x, wexp, ebias, wsplit, sdown, wu, wg2, convb, vecs, consts, keys, out):
    T, D = x.shape
    NT = T // P
    KD = D // P
    E = wexp.shape[1]
    I = P
    SH = sdown.shape[1] * P
    HB = SH // P
    GS = E // NGRP
    NP = E // 2
    assert 2 * CAP == P
    CH = 512
    NC = T // CH
    TC = CH // P
    L = 256
    SEQ = CH // L
    DH = wg2.shape[0]
    CHAINS = 2
    WM = 7
    WR = WM + 6
    SR = 4
    OR = 3
    XR = 8
    SW = L + 2
    XGW = D + E
    NLN = 3

    with ExitStack() as ctx:
        def sb(name, shape, dt=F32):
            return ctx.enter_context(nc.sbuf_tensor(name, shape, dt))

        def sem(name):
            return ctx.enter_context(nc.semaphore(name))

        X = sb("X", [P, NT, D])
        XF = sb("XF", [P, 2, TC, D])
        XN = sb("XN", [P, NT, 2, D], F16)
        XT = sb("XT", [P, 2, KD, T // L * SW + 2], F16)
        S = sb("S", [P, 2, 2 * D])
        HID = sb("HID", [P, 2, HB, CH])
        W = sb("W", [P, WM, 2, KD * I + D])
        W1 = sb("W1", [P, SR, 2, 2, KD * I], F16)
        XG = sb("XG", [P, XR, XGW])
        XD = sb("XD", [P, 3, 2 * KD * P], F16)
        RH = sb("RH", [P, 3, P])
        HT2 = sb("HT2", [P, 3, P])
        YO = sb("YO", [P, 4, D])
        GC = sb("GC", [P, 4])
        GJ = sb("GJ", [P, 4, 2])
        SCR = sb("SCR", [P, 10800])
        raw = HID[:, :, :, :].rearrange("p a b c -> p (a b c)")[:, 0:wsplit.shape[1] + 3 * KD * P]
        w16 = sb("w16", [P, 2, raw.shape[1]], F16)
        sd = sb("sd", [P, HB, D])
        eb = sb("eb", [P, E])
        wus = sb("wus", [P, KD, D])
        cbs = sb("cbs", [2, D])
        cb16 = sb("cb16", [2, 3, D], F16)
        one16 = sb("one16", [2, P], F16)
        wg2s = sb("wg2s", [DH, D])
        vec = sb("vec", [P, vecs.shape[1]])
        cst = sb("cst", [P, consts.shape[1]])
        st = sb("st", [P, NT, 6])
        mv = sb("mv", [P, NT, 2])
        rstd = sb("rstd", [P, NT])
        mh = sb("mh", [P, TC])
        m1 = sb("m1", [P, TC])
        negmean = sb("negmean", [P, NT])
        shift = sb("shift", [P, NT])
        maskb = sb("maskb", [P, NT // 2, 2, E], BF16)
        identb = sb("identb", [P, P], BF16)
        ident16 = sb("ident16", [P, P], F16)
        keyrow = sb("keyrow", [P, T // 2])
        gidx = sb("gidx", [P, NP], U32)
        sidx = sb("sidx", [P, NP], U32)
        zero = sb("zero", [P, 256])

        o = 0
        def cut(n):
            nonlocal o
            o += n
            return cst[:, o - n:o]
        ident = cut(P)
        ones = cut(L)
        parity = cut(2)
        half = cut(1)
        slotno = cut(1)
        sel = cut(4 * NP)
        turned = cut(P)
        bu, bv, bg2 = (vec[:, KD * i:KD * (i + 1)] for i in range(3))
        cw = [vec[:, KD * i:KD * (i + 1)] for i in range(3, 6)]
        first_row = ident[0:2, 0:1]
        bg1 = vec[0:DH, 6 * KD:6 * KD + 1]

        o = 0
        def half_of(n):
            nonlocal o
            o += KD * n
            return w16[:, :, o - KD * n:o].rearrange("p h (k n) -> p h k n", k=KD)
        gw, su, wu16, wv16, wg16 = half_of(E), half_of(SH), half_of(D), half_of(D), half_of(DH)
        assert o == wsplit.shape[1]
        diag = w16[:, :, o:].rearrange("p h (j k n) -> p h j k n", j=3, k=KD)

        def tokens(half, k, t, n, shift=0):
            b = t // L * SW + 2 + t % L + shift
            if n <= L:
                return XT[:, half, k, b:b + n]
            return XT[:, half, k, b:b + n // L * SW].rearrange("p (s l) -> p s l", l=SW)[:, :, 0:L]

        at = 0
        def take(n):
            nonlocal at
            at += n
            return SCR[:, at - n:at]
        hA = take(CH)
        gT = take(KD * CH).rearrange("p (k t) -> p k t", k=KD)
        ug = take(KD * CH).rearrange("p (k t) -> p k t", k=KD)
        vg = take(KD * CH).rearrange("p (k t) -> p k t", k=KD)
        cum = take(KD * CH).rearrange("p (k t) -> p k t", k=KD)
        go = take(2 * KD * CH).rearrange("p (b k t) -> p b k t", b=2, k=KD)
        GATES_AT = at
        gates = take(NT * E).rearrange("p (t e) -> p t e", e=E)
        sco = take(OR * TC * E).rearrange("p (b t e) -> p b t e", b=OR, e=E)
        scb = take(2 * TC * E).rearrange("p (b t e) -> p b t e", b=2, e=E)
        msk = take(TC * (E + 2)).rearrange("p (t e) -> p t e", e=E + 2)
        rept = take(TC * (E + 2)).rearrange("p (t e) -> p t e", e=E + 2)
        tA = take(TC * E)
        tB = take(TC * E // 2)
        tC = take(TC * E // 2)
        sel_sc = take(TC * E).rearrange("p (t e) -> p t e", e=E)
        top = take(TC * 8).rearrange("p (t k) -> p t k", k=8)
        NGM = NGRP + 8 - TOPG
        gsc = take(TC * NGM).rearrange("p (t g) -> p t g", g=NGM)
        grep = take(TC * NGM).rearrange("p (t g) -> p t g", g=NGM)
        gpen = take(TC * NGRP).rearrange("p (t g) -> p t g", g=NGRP)
        sums = take(TC * E // 2).rearrange("p (t e) -> p t e", e=E // 2)
        wsum = take(TC)
        wrec = take(TC)
        slot_a = take(NP)
        slot_b = take(NP)
        SQ = TC // 2 * P
        KEYW = NC * SQ
        keys_at = XG[:, :, :].rearrange("p b w -> p (b w)")
        keyA = keys_at[:, 0:KEYW]
        keyB = keys_at[:, KEYW:2 * KEYW]
        lst = take(CAP)
        upper = take(NP)
        lower = take(NP)
        assert at <= SCR.shape[1], at
        more_w = SCR[:, 0:(WR - WM) * 2 * (KD * I + D)].rearrange("p (b e w) -> p b e w", e=2, w=KD * I + D)
        assert more_w.shape[1] * more_w.shape[2] * more_w.shape[3] <= GATES_AT

        def pair_weights(n):
            b = n % WR
            return W[:, b, :, :] if b < WM else more_w[:, b - WM, :, :]

        PB = 3
        PL = W[:, 0:2 * PB, :, :].rearrange("p (b a) e w -> p b (a e w)", a=2)[:, :, 0:TC * 2 * D].rearrange(
            "p b (t c d) -> p b t c d", t=TC, d=D)

        psT = [ctx.enter_context(nc.psum_tensor(f"psT{b}", [P, 512], F32)) for b in range(2)]
        psA = [ctx.enter_context(nc.psum_tensor(f"psA{b}", [P, 512], F32)) for b in range(2)]
        psC = [ctx.enter_context(nc.psum_tensor(f"psC{b}", [P, 512], F32)) for b in range(2)]
        psR = [ctx.enter_context(nc.psum_tensor(f"psR{b}", [P, 512], F32)) for b in range(2)]

        YR = 2 * T + 2 * P
        table = nc.dram_tensor("table", [T, XGW], F32)
        planes = [nc.dram_tensor(f"plane{c}", [YR, D], F32) for c in range(CHAINS)]

        x_loaded = [sem(f"x_loaded{g}") for g in range(NC)]
        const_loaded = sem("const_loaded")
        raw_loaded = sem("raw_loaded")
        late_loaded = sem("late_loaded")
        idents_made = sem("idents_made")
        diag_made = sem("diag_made")
        hi_made = sem("hi_made")
        lo_made = sem("lo_made")
        xf_ready = sem("xf_ready")
        xhi_ready = sem("xhi_ready")
        pool_added = sem("pool_added")
        dve_added = sem("dve_added")
        w_hi = sem("w_hi")
        w_split = sem("w_split")
        w_loaded = [sem(f"w_loaded{b}") for b in range(WR)]
        T_full = [sem(f"T_full{b}") for b in range(2)]
        T_free = [sem(f"T_free{b}") for b in range(2)]
        A_full = [sem(f"A_full{b}") for b in range(2)]
        A_free = [sem(f"A_free{b}") for b in range(2)]
        C_full = [sem(f"C_full{b}") for b in range(2)]
        C_free = [sem(f"C_free{b}") for b in range(2)]
        dve_step = sem("dve_step")
        act_step = sem("act_step")
        mean_var = [sem(f"mean_var{ln}") for ln in range(NLN)]
        rstd_ready = [sem(f"rstd_ready{ln}") for ln in range(NLN)]
        pool_step = sem("pool_step")
        planes_paired = sem("planes_paired")
        cum_ready = sem("cum_ready")
        xn_ready = [sem(f"xn_ready{ln}") for ln in range(NLN)]
        xt_ready = [sem(f"xt_ready{ln}") for ln in range(NLN)]
        xf_left = sem("xf_left")
        xn_stored = sem("xn_stored")
        gates_ready = sem("gates_ready")
        gates_stored = sem("gates_stored")
        logits_ready = sem("logits_ready")
        scores_ready = sem("scores_ready")
        biased_ready = sem("biased_ready")
        mask_ready = sem("mask_ready")
        maskT_ready = sem("maskT_ready")
        keys_made = sem("keys_made")
        lists_ready = sem("lists_ready")
        slots_made = sem("slots_made")
        slots_copied = sem("slots_copied")
        slots_turned = sem("slots_turned")
        idx_ready = sem("idx_ready")
        hid_ready = sem("hid_ready")
        tail_full = sem("tail_full")
        shared_ready = sem("shared_ready")
        planes_zero = [sem(f"planes_zero{c}") for c in range(CHAINS)]
        const_made = sem("const_made")
        gathered = [sem(f"gathered{b}") for b in range(XR)]
        xd_ready = sem("xd_ready")
        gc_ready = sem("gc_ready")
        relu_ready = sem("relu_ready")
        h_ready = sem("h_ready")
        yo_ready = sem("yo_ready")
        scattered = [sem(f"scattered{c}") for c in range(CHAINS)]
        plane_loaded = [sem(f"plane_loaded{b}") for b in range(PB)]
        plane_used = sem("plane_used")
        hA_ready = sem("hA_ready")
        gT_ready = sem("gT_ready")
        uv_used = sem("uv_used")
        go_ready = sem("go_ready")
        x_final = sem("x_final")
        out_stored = sem("out_stored")

        NPAIR = NT // 2
        TAIL = range(6, 22)
        TAILQ = NPAIR - len(TAIL) // 4
        GP = TC // 2
        order = [(0, g) for g in range(NC)] + [(1, 0)]
        for c in range(NC + 2):
            order += [(1, c + 1)] * (c + 1 < NC) + [(2, c - 2)] * (c >= 2)
        XF_use = {lg: i for i, lg in enumerate(order)}
        T_ln = {lg: i * GP + NP * (lg[0] > 0) for i, lg in enumerate(order)}
        T_ex = [NPAIR, 3 * NPAIR + NP]
        UP = NC * HB
        ATT_A = 1 + 3 * KD
        A_up = [0, UP + NP + NC * ATT_A]
        A_ex = [UP, 2 * UP + NP + NC * ATT_A]
        A_att = UP + NP
        DN = TAILQ
        C_dn = [0, DN + NP + NPAIR]
        C_ex = [DN, 2 * DN + NPAIR + NP]
        C_att = DN + NP

        KEYS_BEFORE = {(1, 0): 1, (1, 2): 2, (1, 3): 3}

        PAIRED = [(0, g) for g in range(1, NC)]

        def shared_added(f, q):
            n = NPAIR // 2
            return (pool_added, f * n + q + 1) if q < n else (dve_added, f * n + q - n + 1)

        def full(sems, n):
            return sems[n % 2], n // 2 + 1

        def scatters(f, i, c):
            return f * len(range(c, NP, CHAINS)) + len(range(c, i, CHAINS))

        x_t = x.rearrange("(t p) d -> p t d", p=P)
        out_t = out.rearrange("(t p) d -> p t d", p=P)
        table_t = table[:, :].rearrange("(t p) w -> p t w", p=P)
        plane_t = [pl[0:2 * T, :].rearrange("(t p c) d -> p t (c d)", p=P, c=2) for pl in planes]

        late = ((eb[:, :], ebias), (sd[:, :, :], sdown), (keyrow[:, :], keys), (wus[:, :, :], wu), (wg2s[:, :], wg2))
        LATE = len(late)

        block = ctx.enter_context(nc.Block())

        @block.sync
        def _(sp):
            sp.dma_start(X[:, 0:TC, :], x_t[:, 0:TC, :]).then_inc(x_loaded[0], 16)
            sp.dma_start(cst[:, :], consts).then_inc(const_loaded, 16)
            sp.dma_start(vec[:, :], vecs).then_inc(const_loaded, 16)
            sp.dma_start(X[:, TC:2 * TC, :], x_t[:, TC:2 * TC, :]).then_inc(x_loaded[1], 16)
            sp.dma_start(raw[:, 0:wsplit.shape[1]], wsplit).then_inc(raw_loaded, 16)
            sp.dma_start(cbs[:, :], convb).then_inc(raw_loaded, 16)
            for g in range(2, NC):
                sp.dma_start(X[:, g * TC:(g + 1) * TC, :], x_t[:, g * TC:(g + 1) * TC, :]).then_inc(x_loaded[g], 16)
            for dst, src in late:
                sp.dma_start(dst, src).then_inc(late_loaded, 16)

            def clear_planes(g):
                rows = YR // P
                a, b = g * rows // NC, (g + 1) * rows // NC
                for c in range(CHAINS):
                    dst = planes[c][:, :].rearrange("(p r) d -> p r d", p=P)[:, a:b, :]
                    sp.dma_start(dst, zero[:, None, :].to_broadcast([P, b - a, D])).then_inc(planes_zero[c], 16)

            def load_weights(f, i):
                n = f * NP + i
                if n >= WR:
                    b, a = divmod(n - WR, NP)
                    sp.wait_ge(*full(C_full, C_ex[b] + a))
                    sp.wait_ge(w_split, n - WR + 1)
                if f:
                    sp.wait_ge(plane_used, NC * CHAINS)
                if f and n % WR >= WM:
                    sp.wait_ge(*full(C_full, C_att + NPAIR - 1))
                for e in range(2):
                    sp.dma_start(pair_weights(n)[:, e, :], wexp[:, 2 * i + e, :]).then_inc(w_loaded[n % WR], 16)

            for f in range(2):
                if f == 0:
                    sp.wait_ge(const_made, 1)
                for g in range(NC):
                    if f == 0:
                        clear_planes(g)
                    sp.wait_ge(xn_ready[2 * f], g + 1)
                    sp.dma_start(table_t[:, g * TC:(g + 1) * TC, 0:D],
                                 XN[:, g * TC:(g + 1) * TC, :, :].rearrange("p t h d -> p t (h d)").bitcast(F32)
                                 ).then_inc(xn_stored, 16)
                for q in range(WR):
                    load_weights(f, q)
                sp.wait_ge(gates_ready, NC * (f + 1))
                sp.dma_start(table_t[:, :, D:XGW], gates[:, :, :]).then_inc(gates_stored, 16)
                for q in range(WR, NP):
                    load_weights(f, q)
                for g in range(NC):
                    for c in range(CHAINS):
                        if g == 0:
                            sp.wait_ge(scattered[c], 16 * scatters(f, NP, c))
                        n = (f * NC + g) * CHAINS + c
                        if n >= PB:
                            sp.wait_ge(plane_used, n - PB + 1)
                        sp.dma_start(PL[:, n % PB, :, :, :],
                                     plane_t[c][:, g * TC:(g + 1) * TC, :].rearrange("p t (c d) -> p t c d", c=2)
                                     ).then_inc(plane_loaded[n % PB], 16)
                if f == 0:
                    sp.wait_ge(plane_used, NC * CHAINS)
                    for g in range(NC):
                        clear_planes(g)
            for g in range(NC):
                sp.wait_ge(x_final, g + 1)
                sp.dma_start(out_t[:, g * TC:(g + 1) * TC, :], X[:, g * TC:(g + 1) * TC, :]).then_inc(out_stored, 16)
            sp.wait_ge(out_stored, 16 * NC)

        @block.gpsimd
        def _(pool):
            pool.memset(zero[:, :], 0.0).then_inc(const_made, 1)
            pool.memset(mh[:, :], -0.5)
            pool.memset(m1[:, :], -1.0)
            pool.memset(one16[:, :], 1.0)
            for a in (0, 1):
                pool.memset(XT[:, :, :, a:a + T // L * SW + 1:SW], 0.0)
            pool.memset(XG[:, :, :], 0.0).then_inc(const_made, 1)
            pool.wait_ge(const_made, 2)

            steps = [0]

            def link(ins):
                steps[0] += 1
                ins.then_inc(pool_step, 1)
                pool.wait_ge(pool_step, steps[0])

            def roots(ln, g):
                pool.wait_ge(mean_var[ln], g + 1)
                gs = slice(g * TC, (g + 1) * TC)
                link(pool.tensor_tensor(rstd[:, gs], mv[:, gs, 1], mh[:, :], ALU.pow))
                pool.tensor_tensor(shift[:, gs], negmean[:, gs], rstd[:, gs], ALU.mult).then_inc(rstd_ready[ln], 1)

            def low_half(ln, g):
                m = XF_use[ln, g]
                pool.wait_ge(xhi_ready, m + 1)
                pool.tensor_tensor(XN[:, g * TC:(g + 1) * TC, 1, :], XF[:, m % 2, :, :],
                                   XN[:, g * TC:(g + 1) * TC, 0, :], ALU.subtract).then_inc(xn_ready[ln], 1)
                pool.wait_ge(xn_ready[ln], g + 1)
                pool.nop().then_inc(xf_left, 1)

            def add_shared(f, c):
                for q in range(c * GP, (c + 1) * GP):
                    n = f * NPAIR + q
                    pool.wait_ge(shared_ready, n + 1)
                    xs = X[:, 2 * q:2 * q + 2, :].rearrange("p t d -> p (t d)")
                    pool.tensor_tensor(xs, xs, S[:, n % 2, :], ALU.add).then_inc(pool_added, 1)

            def biased_scores(f, g):
                n = f * NC + g
                pool.wait_ge(scores_ready, n + 1)
                if n == 0:
                    pool.wait_ge(late_loaded, 16 * LATE)
                if n >= 2:
                    pool.wait_ge(mask_ready, n - 1)
                pool.tensor_tensor(scb[:, n % 2, :, :], sco[:, n % OR, :, :], eb[:, None, :].to_broadcast([P, TC, E]),
                                   ALU.add).then_inc(biased_ready, 1)

            def token_gates(f, g):
                n = f * NC + g
                gs = slice(g * TC, (g + 1) * TC)
                q = g * TC // 2
                pool.wait_ge(mask_ready, n + 1)
                if n:
                    pool.wait_ge(gates_ready, n)
                halves = lambda z: z.rearrange("p (h t) e -> p h t e", h=2)
                link(pool.tensor_tensor(halves(sel_sc), maskb[:, q:q + TC // 2, :, :].rearrange("p t h e -> p h t e"),
                                        halves(sco[:, n % OR, :, :]), ALU.mult))
                link(pool.tensor_tensor(sums[:, :, :], sel_sc[:, :, 0:E // 2], sel_sc[:, :, E // 2:E], ALU.add))
                w = E // 4
                while w:
                    link(pool.tensor_tensor(sums[:, :, 0:w], sums[:, :, 0:w], sums[:, :, w:2 * w], ALU.add))
                    w //= 2
                link(pool.tensor_scalar(wsum, sums[:, :, 0], 1e-20, 1 / (ROUTE_SCALE * HALF), ALU.add, ALU.mult))
                link(pool.tensor_tensor(wrec, wsum, m1[:, :], ALU.pow))
                if f and g == 0:
                    pool.wait_ge(gates_stored, 16)
                pool.tensor_tensor(gates[:, gs, :], sel_sc, wrec[:, :, None].to_broadcast([P, TC, E]), ALU.mult
                                   ).then_inc(gates_ready, 1)

            roots(0, 0)
            roots(0, 1)
            low_half(0, 0)
            low_half(0, 1)
            roots(0, 2)
            biased_scores(0, 0)
            roots(0, 3)
            low_half(0, 2)
            biased_scores(0, 1)
            token_gates(0, 0)
            biased_scores(0, 2)
            low_half(0, 3)
            biased_scores(0, 3)
            token_gates(0, 1)
            token_gates(0, 2)
            add_shared(0, 0)
            token_gates(0, 3)
            add_shared(0, 1)
            for f in range(2):
                if f:
                    token_gates(1, NC - 1)
                    add_shared(f, 0)
                    add_shared(f, 1)
                pool.wait_ge(idx_ready, f + 1)
                pool.wait_ge(xn_stored, 16 * NC * (f + 1))
                pool.wait_ge(gates_stored, 16 * (f + 1))

                def gather(i):
                    n = f * NP + i
                    if n >= XR:
                        pool.wait_ge(*full(T_full, T_ex[f] + i - XR if i >= XR else T_ex[0] + NP - XR + i))
                        pool.wait_ge(gc_ready, n - XR + 1)
                    pool.indirect_dma_start(XG[:, n % XR, :], None, table[:, :],
                                            bass.IndirectOffsetOnAxis(ap=gidx[:, i:i + 1], axis=0),
                                            bounds_check=T - 1, oob_is_err=False).then_inc(gathered[n % XR], 16)

                for i in range(XR):
                    gather(i)
                for c in range(CHAINS):
                    pool.wait_ge(planes_zero[c], 16 * NC * (f + 1))
                for i in range(NP):
                    n = f * NP + i
                    pool.wait_ge(yo_ready, n + 1)
                    c = i % CHAINS
                    m = scatters(f, i, c)
                    if m:
                        pool.wait_ge(scattered[c], 16 * m)
                    pool.indirect_dma_start(planes[c][:, :], bass.IndirectOffsetOnAxis(ap=sidx[:, i:i + 1], axis=0),
                                            YO[:, n % 4, :], None, bounds_check=YR - 1, oob_is_err=True,
                                            compute_op=ALU.add).then_inc(scattered[c], 16)
                    if i + XR < NP:
                        gather(i + XR)

                def pair_planes(g):
                    n = (f * NC + g) * CHAINS + 1
                    pool.wait_ge(plane_loaded[n % PB], 16 * (n // PB + 1))
                    pool.tensor_tensor(PL[:, n % PB, :, 0, :], PL[:, n % PB, :, 0, :], PL[:, n % PB, :, 1, :],
                                       ALU.add).then_inc(planes_paired, 1)

                if f == 0:
                    roots(1, 0)
                    pair_planes(1)
                    low_half(1, 0)
                    roots(1, 1)
                    pair_planes(2)
                    roots(1, 2)
                    pair_planes(3)
                    low_half(1, 1)
                    for c in range(NC + 2):
                        if c >= 2:
                            low_half(2, c - 2)
                        if c > 2:
                            biased_scores(1, c - 2)
                        if c < NC:
                            pool.wait_ge(cum_ready, c + 1)
                            if c >= 2:
                                pool.wait_ge(*full(C_full, C_att + (c - 1) * TC // 2 - 1))
                            pool.tensor_tensor(go[:, c % 2, :, :], cum[:, :, :], vg[:, :, :], ALU.mult
                                               ).then_inc(go_ready, 1)
                        if c == 0:
                            roots(1, 3)
                        if c <= 1:
                            low_half(1, c + 2)
                        if 1 <= c <= NC:
                            roots(2, c - 1)
                        if c == 2:
                            biased_scores(1, 0)
                        if c >= 3:
                            token_gates(1, c - 3)

        @block.tensor
        def _(pe):
            def products(out, lhsT, rhs, ks, first=True, last=True):
                todo = [(a, b, k) for a, b in PASSES for k in range(ks)]
                for i, (a, b, k) in enumerate(todo):
                    mm = pe.matmul(out, lhsT(a, k), rhs(b, k), start=first and i == 0, stop=last and i == len(todo) - 1)
                return mm

            def layernorm_T(ln, g):
                pe.wait_ge(xn_ready[ln], g + 1)
                for q in range(g * TC // 2, (g + 1) * TC // 2):
                    n = T_ln[ln, g] + q - g * GP
                    if n >= 2:
                        pe.wait_ge(T_free[n % 2], n // 2)
                    pt = psT[n % 2][:, :].bitcast(F16)
                    for h in range(2):
                        for k in range(KD):
                            for j in range(2):
                                b = ((h * KD + k) * 2 + j) * P
                                mm = pe.transpose(pt[:, b:b + P], XN[:, 2 * q + j, h, k * P:(k + 1) * P], ident16[:, :])
                    mm.then_inc(T_full[n % 2], 1)

            def logits(f, g):
                if f * NC + g:
                    pe.wait_ge(scores_ready, f * NC + g)
                if f and g == 0:
                    pe.wait_ge(shared_ready, NPAIR)
                for q in range(g * TC // 2, (g + 1) * TC // 2):
                    pe.wait_ge(xt_ready[2 * f], q + 1)
                    for j in (2 * q, 2 * q + 1):
                        o = j % (2 * TC) * E
                        mm = products(psR[0][:, o:o + E], lambda h, k: tokens(h, k, j * P, P),
                                      lambda h, k: gw[:, h, k, :], KD)
                    mm.then_inc(logits_ready, 1)

            def up(f, c):
                for h in range(HB):
                    n = A_up[f] + c * HB + h
                    if n >= 2:
                        pe.wait_ge(A_free[n % 2], n // 2)
                    products(psA[n % 2][:, :], lambda a, k: su[:, a, k, h * P:(h + 1) * P],
                             lambda b, k: tokens(b, k, c * CH, CH), KD).then_inc(A_full[n % 2], 1)

            def down(f, c, part=range(TC // 2)):
                pe.wait_ge(hid_ready, f * UP + (c + 1) * HB)
                for q in part:
                    n = C_dn[f] + c * TC // 2 + q
                    if n >= 2:
                        pe.wait_ge(C_free[n % 2], n // 2)
                    for j in range(2):
                        tt = (2 * q + j) * P
                        for h in range(HB):
                            mm = pe.matmul(psC[n % 2][:, j * D:(j + 1) * D], HID[:, c % 2, h, tt:tt + P], sd[:, h, :],
                                           start=(h == 0), stop=(h == HB - 1))
                    mm.then_inc(C_full[n % 2], 1)

            def down_tail(f, j):
                if j == 0:
                    pe.wait_ge(hid_ready, (f + 1) * UP)
                    pe.wait_ge(idx_ready, f + 1)
                q, part = divmod(j, 4)
                if q >= 2 and part == 0:
                    pe.wait_ge(shared_ready, f * NPAIR + TAILQ + q - 1)
                t = 2 * TAILQ + j // 2
                w = D // 2
                for h in range(HB):
                    mm = pe.matmul(psR[q % 2][:, part * w:(part + 1) * w],
                                   HID[:, t // TC % 2, h, t % TC * P:(t % TC + 1) * P],
                                   sd[:, h, j % 2 * w:(j % 2 + 1) * w], start=(h == 0), stop=(h == HB - 1))
                mm.then_inc(tail_full, 1)

            def mask_T(f, g):
                pe.wait_ge(mask_ready, f * NC + g + 1)
                if (f, g) in KEYS_BEFORE:
                    pe.wait_ge(keys_made, KEYS_BEFORE[f, g])
                pb = psR[1][:, :].bitcast(BF16)
                for t in range(g * TC // 2, (g + 1) * TC // 2):
                    mm = pe.transpose(pb[:, t * P:(t + 1) * P], maskb[:, t, :, :].rearrange("p h e -> p (h e)"),
                                      identb[:, :])
                mm.then_inc(maskT_ready, 1)

            def list_slots(f):
                pe.wait_ge(lists_ready, f + 1)
                for h in range(2):
                    mm = pe.matmul(psR[1][h * CAP:(h + 1) * CAP, 0:2 * NP], lst[:, 0:CAP],
                                   sel[:, h * 2 * NP:(h + 1) * 2 * NP], start=True, stop=True)
                mm.then_inc(slots_made, 1)

            def turn_slots(f):
                pe.wait_ge(slots_copied, f + 1)
                pe.matmul(psR[0][:, 0:NP], turned, lower, start=True, stop=True).then_inc(slots_turned, 1)

            def turn(f, i):
                n = f * NP + i
                pe.wait_ge(gathered[n % XR], 16 * (n // XR + 1))
                u = T_ex[f] + i
                pe.wait_ge(T_free[u % 2], u // 2)
                pt, rows = psT[u % 2][:, :].bitcast(F16), XG[:, n % XR, 0:D].bitcast(F16)
                for b in range(2 * KD):
                    mm = pe.transpose(pt[:, b * P:(b + 1) * P], rows[:, b * P:(b + 1) * P], ident16[:, :])
                mm.then_inc(T_full[u % 2], 1)

            def first(f, i):
                n = f * NP + i
                pe.wait_ge(w_split, n + 1)
                pe.wait_ge(xd_ready, n + 1)
                u = A_ex[f] + i
                pe.wait_ge(A_free[u % 2], u // 2)
                for s in range(2):
                    mm = products(psA[u % 2][:, s * CAP:(s + 1) * CAP],
                                  lambda a, k: W1[:, n % SR, a, s, k * I:(k + 1) * I],
                                  lambda b, k: XD[:, n % 3, (b * KD + k) * P + s * CAP:(b * KD + k) * P + (s + 1) * CAP], KD)
                mm.then_inc(A_full[u % 2], 1)

            def second(f, i):
                n = f * NP + i
                pe.wait_ge(h_ready, n + 1)
                u = C_ex[f] + i
                pe.wait_ge(C_free[u % 2], u // 2)
                for s in range(2):
                    mm = pe.matmul(psC[u % 2][s * CAP:(s + 1) * CAP, 0:D], HT2[:, n % 3, s * CAP:(s + 1) * CAP],
                                   pair_weights(n)[:, s, KD * I:], start=True, stop=True)
                mm.then_inc(C_full[u % 2], 1)

            def experts(f):
                for s in range(NP + 3):
                    if s < NP:
                        turn(f, s)
                    if 1 <= s <= NP:
                        first(f, s - 1)
                    if s in TAIL:
                        down_tail(f, TAIL.index(s))
                    if s >= 3:
                        second(f, s - 3)

            def attention(c):
                n = [A_att + c * ATT_A]

                def slot():
                    u = n[0]
                    n[0] += 1
                    pe.wait_ge(A_free[u % 2], u // 2)
                    return u
                pe.wait_ge(xt_ready[1], (c + 1) * TC // 2)
                u = slot()
                products(psA[u % 2][0:DH, :], lambda a, k: wg16[:, a, k, :], lambda b, k: tokens(b, k, c * CH, CH),
                         KD).then_inc(A_full[u % 2], 1)
                pe.wait_ge(hA_ready, c + 1)
                for r in range(KD):
                    u = slot()
                    pe.matmul(psA[u % 2][:, :], wg2s[:, r * P:(r + 1) * P], hA[0:DH, :],
                              start=True, stop=True).then_inc(A_full[u % 2], 1)
                for w in (wu16, wv16):
                    for r in range(KD):
                        u = slot()
                        products(psA[u % 2][:, :], lambda a, k: w[:, a, k, r * P:(r + 1) * P],
                                 lambda b, k: tokens(b, k, c * CH, CH), KD).then_inc(A_full[u % 2], 1)

            def att_project(c):
                pe.wait_ge(go_ready, c + 1)
                for q in range(TC // 2):
                    u = C_att + c * TC // 2 + q
                    pe.wait_ge(C_free[u % 2], u // 2)
                    for j in range(2):
                        tt = (2 * q + j) * P
                        pe.matmul(psC[u % 2][:, j * D:(j + 1) * D], one16[:, :], cb16[:, 2, :], start=True, stop=False)
                        for k in range(KD):
                            for tap in range(3):
                                products(psC[u % 2][:, j * D + k * P:j * D + (k + 1) * P],
                                         lambda a, _: tokens(a, k, c * CH + tt, P, tap - 1),
                                         lambda b, _: diag[:, b, tap, k, :], 1, False, False)
                        for r in range(KD):
                            mm = pe.matmul(psC[u % 2][:, j * D:(j + 1) * D], go[:, c % 2, r, tt:tt + P],
                                           wus[:, r, :], start=False, stop=(r == KD - 1))
                    mm.then_inc(C_full[u % 2], 1)

            pe.wait_ge(idents_made, 2)
            layernorm_T(0, 0)
            pe.wait_ge(lo_made, 1)
            logits(0, 0)
            layernorm_T(0, 1)
            logits(0, 1)
            up(0, 0)
            layernorm_T(0, 2)
            logits(0, 2)
            mask_T(0, 0)
            layernorm_T(0, 3)
            logits(0, 3)
            mask_T(0, 1)
            up(0, 1)
            mask_T(0, 2)
            mask_T(0, 3)
            pe.wait_ge(late_loaded, 16 * LATE)
            down(0, 0)
            up(0, 2)
            down(0, 1)
            list_slots(0)
            turn_slots(0)
            up(0, 3)
            experts(0)
            layernorm_T(1, 0)
            for c in range(NC + 2):
                if c < NC:
                    attention(c)
                if c + 1 < NC:
                    layernorm_T(1, c + 1)
                if c == NC - 1:
                    layernorm_T(2, c - 2)
                    logits(1, c - 2)
                if 1 <= c <= NC:
                    att_project(c - 1)
                if c == NC - 1:
                    mask_T(1, 0)
                    mask_T(1, 1)
                if c == NC + 1:
                    mask_T(1, 2)
                    up(1, 1)
                if c >= 2 and c != NC - 1:
                    layernorm_T(2, c - 2)
                    logits(1, c - 2)
                if c == NC:
                    up(1, 0)
            down(1, 0)
            mask_T(1, 3)
            up(1, 2)
            down(1, 1, [0])
            list_slots(1)
            turn_slots(1)
            down(1, 1, [1])
            up(1, 3)
            experts(1)

        @block.scalar
        def _(act):
            steps = [0]

            def link(ins):
                steps[0] += 1
                ins.then_inc(act_step, 1)
                act.wait_ge(act_step, steps[0])

            def normal(ln, g):
                m = XF_use[ln, g]
                act.wait_ge(rstd_ready[ln], g + 1)
                if m >= 2:
                    act.wait_ge(xf_left, m - 1)
                if ln:
                    act.wait_ge(*full(T_full, T_ln[ln - 1, g] + GP - 1))
                    if ln == 1:
                        act.wait_ge(xn_stored, 16 * NC)
                for j in range(TC):
                    t = g * TC + j
                    ins = act.activation(XF[:, m % 2, j, :], X[:, t, :], ACT.Identity, bias=shift[:, t:t + 1],
                                         scale=rstd[:, t:t + 1])
                ins.then_inc(xf_ready, 1)
                act.wait_ge(xf_ready, m + 1)
                act.activation(XN[:, g * TC:(g + 1) * TC, 0, :], XF[:, m % 2, :, :], ACT.Copy).then_inc(xhi_ready, 1)

            def scores(f, g):
                act.wait_ge(logits_ready, f * NPAIR + (g + 1) * TC // 2)
                n = f * NC + g
                if n >= OR:
                    act.wait_ge(gates_ready, n - OR + 1)
                o = g % 2 * TC * E
                act.activation(sco[:, n % OR, :, :], psR[0][:, o:o + TC * E].rearrange("p (t e) -> p t e", e=E),
                               ACT.Sigmoid).then_inc(scores_ready, 1)

            def xt_copy(ln, g):
                for q in range(g * TC // 2, (g + 1) * TC // 2):
                    n = T_ln[ln, g] + q - g * GP
                    act.wait_ge(*full(T_full, n))
                    act.copy(XT[:, :, :, q * SW + 2:(q + 1) * SW].rearrange("p h k l -> p (h k) l").bitcast(F32),
                             psT[n % 2][:, :].rearrange("p (a t) -> p a t", a=2 * KD)).then_inc(xt_ready[ln], 1)
                    act.wait_ge(xt_ready[ln], q + 1)
                    act.nop().then_inc(T_free[n % 2], 1)

            def hidden(f, c):
                for h in range(HB):
                    n = A_up[f] + c * HB + h
                    act.wait_ge(*full(A_full, n))
                    link(act.activation(HID[:, c % 2, h, :], psA[n % 2][:, :], ACT.Relu))
                    act.nop().then_inc(A_free[n % 2], 1)
                    act.activation(HID[:, c % 2, h, :], HID[:, c % 2, h, :], ACT.Square).then_inc(hid_ready, 1)

            def leave(f, q, bank):
                z = f * NPAIR + q
                if z >= 2:
                    act.wait_ge(*shared_added((z - 2) // NPAIR, (z - 2) % NPAIR))
                return act.activation(S[:, z % 2, :], bank[:, :], ACT.Copy, scale=HALF)

            def shared_out(f, c):
                for q in range(GP):
                    n = C_dn[f] + c * GP + q
                    act.wait_ge(*full(C_full, n))
                    leave(f, c * GP + q, psC[n % 2]).then_inc(shared_ready, 1)
                    act.wait_ge(shared_ready, f * NPAIR + c * GP + q + 1)
                    act.nop().then_inc(C_free[n % 2], 1)

            def weights_hi(f, i):
                m = f * NP + i
                act.wait_ge(w_loaded[m % WR], 32 * (m // WR + 1))
                if m >= SR:
                    b, a = divmod(m - SR, NP)
                    act.wait_ge(*full(A_full, A_ex[b] + a))
                act.activation(W1[:, m % SR, 0, :, :], pair_weights(m)[:, :, 0:KD * I], ACT.Copy).then_inc(w_hi, 1)

            def experts(f):
                def relu(i):
                    n = f * NP + i
                    u = A_ex[f] + i
                    act.wait_ge(*full(A_full, u))
                    if n >= 3:
                        act.wait_ge(h_ready, n - 2)
                    act.activation(RH[:, n % 3, :], psA[u % 2][:, 0:P], ACT.Relu).then_inc(relu_ready, 1)
                    act.wait_ge(relu_ready, n + 1)
                    act.nop().then_inc(A_free[u % 2], 1)

                def gated(i):
                    n = f * NP + i
                    u = C_ex[f] + i
                    act.wait_ge(*full(C_full, u))
                    act.wait_ge(gc_ready, n + 1)
                    if n >= 4:
                        b, a = divmod(n - 4, NP)
                        act.wait_ge(scattered[a % CHAINS], 16 * (scatters(b, a, a % CHAINS) + 1))
                    act.activation(YO[:, n % 4, :], psC[u % 2][:, 0:D], ACT.Copy, scale=GC[:, n % 4:n % 4 + 1]
                                   ).then_inc(yo_ready, 1)
                    act.wait_ge(yo_ready, n + 1)
                    act.nop().then_inc(C_free[u % 2], 1)

                for s in range(NP + 3):
                    if 1 <= s <= NP:
                        relu(s - 1)
                    if s - 1 in TAIL[3::4]:
                        q = TAIL.index(s - 1) // 4
                        act.wait_ge(tail_full, f * len(TAIL) + 4 * q + 4)
                        leave(f, TAILQ + q, psR[q % 2]).then_inc(shared_ready, 1)
                    if s >= 3:
                        gated(s - 3)
                    if SR <= s + 2 < NP:
                        weights_hi(f, s + 2)

            def attention(c):
                n = A_att + c * ATT_A
                act.wait_ge(*full(A_full, n))
                act.activation(hA[0:DH, :], psA[n % 2][0:DH, :], ACT.Relu, bias=bg1).then_inc(hA_ready, 1)
                act.wait_ge(hA_ready, c + 1)
                act.nop().then_inc(A_free[n % 2], 1)
                if c >= 1:
                    act.wait_ge(uv_used, 2 * KD * c)
                for r in range(KD):
                    u = n + 1 + r
                    act.wait_ge(*full(A_full, u))
                    act.activation(gT[:, r, :], psA[u % 2][:, :], ACT.Sigmoid, bias=bg2[:, r:r + 1]).then_inc(gT_ready, 1)
                    act.wait_ge(gT_ready, c * KD + r + 1)
                    act.nop().then_inc(A_free[u % 2], 1)

            normal(0, 0)
            act.wait_ge(raw_loaded, 32)
            act.wait_ge(diag_made, 1)
            act.activation(w16[:, 0, :], raw, ACT.Copy).then_inc(hi_made, 1)
            act.activation(cb16[:, 0, :], cbs[:, :], ACT.Copy).then_inc(hi_made, 1)
            act.wait_ge(const_made, 2)
            xt_copy(0, 0)
            normal(0, 1)
            scores(0, 0)
            xt_copy(0, 1)
            normal(0, 2)
            scores(0, 1)
            act.wait_ge(lo_made, 1)
            hidden(0, 0)
            xt_copy(0, 2)
            normal(0, 3)
            scores(0, 2)
            xt_copy(0, 3)
            scores(0, 3)
            hidden(0, 1)
            shared_out(0, 0)
            hidden(0, 2)
            shared_out(0, 1)
            for i in range(SR):
                weights_hi(0, i)
            hidden(0, 3)
            experts(0)
            normal(1, 0)
            xt_copy(1, 0)
            act.wait_ge(const_loaded, 32)
            for c in range(NC + 2):
                if c < NC:
                    attention(c)
                if c + 1 < NC:
                    normal(1, c + 1)
                    xt_copy(1, c + 1)
                if c >= 2:
                    normal(2, c - 2)
                if c == NC + 1:
                    hidden(1, 1)
                if c >= 2:
                    xt_copy(2, c - 2)
                    scores(1, c - 2)
                if c == NC:
                    hidden(1, 0)
            shared_out(1, 0)
            hidden(1, 2)
            shared_out(1, 1)
            for i in range(SR):
                weights_hi(1, i)
            hidden(1, 3)
            experts(1)

        @block.vector
        def _(dve):
            steps = [0]

            def link(ins):
                steps[0] += 1
                ins.then_inc(dve_step, 1)
                dve.wait_ge(dve_step, steps[0])

            def stats(ln, g):
                for j in range(g * TC, (g + 1) * TC):
                    ins = dve.bn_stats(st[:, j, :], X[:, j, :])
                link(ins)
                for j in range(g * TC, (g + 1) * TC):
                    ins = dve.bn_aggr(mv[:, j, :], st[:, j, :])
                link(ins)
                gs = slice(g * TC, (g + 1) * TC)
                dve.tensor_scalar(negmean[:, gs], mv[:, gs, 0], -1.0, None, ALU.mult)
                dve.tensor_scalar(mv[:, gs, 1], mv[:, gs, 1], EPS, None, ALU.add).then_inc(mean_var[ln], 1)

            def constants():
                dve.wait_ge(const_loaded, 32)
                dve.tensor_copy(identb[:, :], ident).then_inc(idents_made, 1)
                dve.tensor_copy(ident16[:, :], ident).then_inc(idents_made, 1)
                for j in range(3):
                    for k in range(KD):
                        b = wsplit.shape[1] + (j * KD + k) * P
                        ins = dve.tensor_scalar(raw[:, b:b + P], ident, cw[j][:, k:k + 1], None, ALU.mult)
                ins.then_inc(diag_made, 1)

            def route(f, g):
                n = f * NC + g
                dve.wait_ge(biased_ready, n + 1)
                dve.memset(msk[:, :, E:E + 2], 2 * FAR)
                dve.memset(gsc[:, :, NGRP:NGM], 2 * FAR)
                a = scb[:, n % 2, :, :].rearrange("p t (g s) -> p (t g) s", s=GS)
                NG = TC * NGRP
                q = NG * 4
                hi = tA[:, 0:q].rearrange("p (g s) -> p g s", s=4)
                lo = tA[:, q:2 * q].rearrange("p (g s) -> p g s", s=4)
                dve.tensor_tensor(hi, a[:, :, 0:4], a[:, :, 4:8], ALU.max)
                link(dve.tensor_tensor(lo, a[:, :, 0:4], a[:, :, 4:8], ALU.min))
                q = NG * 2
                h2 = tB[:, 0:q].rearrange("p (g s) -> p g s", s=2)
                m2 = tB[:, q:2 * q].rearrange("p (g s) -> p g s", s=2)
                l2 = tC[:, 0:q].rearrange("p (g s) -> p g s", s=2)
                n2 = tC[:, q:2 * q].rearrange("p (g s) -> p g s", s=2)
                dve.tensor_tensor(h2, hi[:, :, 0:2], hi[:, :, 2:4], ALU.max)
                dve.tensor_tensor(m2, hi[:, :, 0:2], hi[:, :, 2:4], ALU.min)
                link(dve.tensor_tensor(l2, lo[:, :, 0:2], lo[:, :, 2:4], ALU.max))
                link(dve.tensor_tensor(n2, m2, l2, ALU.max))
                h1, w1, l1, n1 = (tA[:, NG * i:NG * (i + 1)] for i in range(4))
                dve.tensor_tensor(h1, h2[:, :, 0], h2[:, :, 1], ALU.max)
                dve.tensor_tensor(w1, h2[:, :, 0], h2[:, :, 1], ALU.min)
                link(dve.tensor_tensor(l1, n2[:, :, 0], n2[:, :, 1], ALU.max))
                link(dve.tensor_tensor(n1, w1, l1, ALU.max))
                link(dve.tensor_tensor(gsc[:, :, 0:NGRP], h1.rearrange("p (t g) -> p t g", g=NGRP),
                                       n1.rearrange("p (t g) -> p t g", g=NGRP), ALU.add))
                for t in range(TC):
                    ins = dve.max(top[:, t, :], gsc[:, t, 0:NGRP])
                link(ins)
                link(dve.memset(top[:, :, TOPG:8], 2 * FAR))
                for t in range(TC):
                    ins = dve.match_replace(grep[:, t, :], top[:, t, :], gsc[:, t, :], FAR)
                link(ins)
                link(dve.tensor_scalar(gpen[:, :, :], grep[:, :, 0:NGRP], FAR, -FAR, ALU.not_equal, ALU.mult))
                link(dve.tensor_tensor(msk[:, :, 0:E].rearrange("p t (g s) -> p t g s", s=GS),
                                       scb[:, n % 2, :, :].rearrange("p t (g s) -> p t g s", s=GS),
                                       gpen[:, :, :, None].to_broadcast([P, TC, NGRP, GS]), ALU.add))
                for t in range(TC):
                    ins = dve.max(top[:, t, :], msk[:, t, 0:E])
                link(ins)
                link(dve.memset(top[:, :, TOPK:8], 2 * FAR))
                for t in range(TC):
                    ins = dve.match_replace(rept[:, t, :], top[:, t, :], msk[:, t, :], FAR)
                link(ins)
                q = g * TC // 2
                dve.tensor_scalar(maskb[:, q:q + TC // 2, :, :].rearrange("p t h e -> p h t e"),
                                  rept[:, :, 0:E].rearrange("p (h t) e -> p h t e", h=2), FAR, None, ALU.is_equal
                                  ).then_inc(mask_ready, 1)

            keys = [0]

            def search(f, g0, g1):
                old = CAP if g0 else 0
                if g0:
                    link(dve.tensor_copy(keyA[:, 0:CAP], lst[:, 0:CAP]))
                dve.wait_ge(maskT_ready, f * NC + g1)
                end = old + (g1 - g0) * SQ
                dve.tensor_tensor(keyA[:, old:end], psR[1][:, :].bitcast(BF16)[:, g0 * SQ:g1 * SQ],
                                  keyrow[:, g0 * SQ:g1 * SQ], ALU.mult).then_inc(keys_made, 1)
                keys[0] += 1
                dve.wait_ge(keys_made, keys[0])
                a, b = keyA[:, 0:end], keyB[:, 0:end]
                for r in range(CAP // 8):
                    link(dve.max(lst[:, r * 8:(r + 1) * 8], a))
                    if r < CAP // 8 - 1:
                        link(dve.match_replace(b, lst[:, r * 8:(r + 1) * 8], a, 0.0))
                        a, b = b, a

            def slots(f):
                dve.nop().then_inc(lists_ready, 1)
                dve.wait_ge(slots_made, f + 1)
                dve.tensor_copy(upper, psR[1][:, 0:NP])
                link(dve.tensor_copy(lower, psR[1][:, NP:2 * NP]))
                dve.nop().then_inc(slots_copied, 1)
                dve.wait_ge(slots_turned, f + 1)
                link(dve.tensor_tensor(upper, upper, psR[0][:, 0:NP], ALU.max))
                tok, emp = slot_a, slot_b
                key = upper
                dve.tensor_scalar(gidx[:, :], key, -1.0, float(T), ALU.mult, ALU.add)
                dve.tensor_scalar(tok, key, -2.0, 2.0 * T, ALU.mult, ALU.add)
                link(dve.tensor_scalar(emp, key, 0.0, slotno, ALU.is_equal, ALU.mult))
                link(dve.tensor_tensor(tok, tok, emp, ALU.add))
                link(dve.tensor_scalar(sidx[:, :], tok, half, None, ALU.add))
                dve.nop().then_inc(idx_ready, 1)

            def experts(f):
                def xd(i):
                    n = f * NP + i
                    u = T_ex[f] + i
                    dve.wait_ge(*full(T_full, u))
                    if n >= 3:
                        m = A_ex[f] + i - 3 if i >= 3 else A_ex[0] + NP - 3 + i
                        dve.wait_ge(*full(A_full, m))
                    dve.tensor_copy(XD[:, n % 3, :].bitcast(F32), psT[u % 2][:, 0:KD * P]).then_inc(xd_ready, 1)
                    if n >= 4:
                        dve.wait_ge(yo_ready, n - 3)
                    dve.tensor_tensor_reduce(out=GJ[:, n % 4, :], in0=XG[:, n % XR, D + 2 * i:D + 2 * i + 2], in1=parity,
                                             scale=1.0, scalar=0.0, op0=ALU.mult, op1=ALU.add,
                                             accum_out=GC[:, n % 4:n % 4 + 1]).then_inc(gc_ready, 1)
                    dve.wait_ge(xd_ready, n + 1)
                    dve.nop().then_inc(T_free[u % 2], 1)

                def square(i):
                    n = f * NP + i
                    dve.wait_ge(relu_ready, n + 1)
                    if n >= 3:
                        m = C_ex[f] + i - 3 if i >= 3 else C_ex[0] + NP - 3 + i
                        dve.wait_ge(*full(C_full, m))
                    dve.tensor_tensor(HT2[:, n % 3, :], RH[:, n % 3, :], RH[:, n % 3, :], ALU.mult).then_inc(h_ready, 1)

                def weights_lo(i):
                    m = f * NP + i
                    dve.wait_ge(w_hi, m + 1)
                    dve.tensor_tensor(W1[:, m % SR, 1, :, :], pair_weights(m)[:, :, 0:KD * I], W1[:, m % SR, 0, :, :],
                                      ALU.subtract).then_inc(w_split, 1)

                def add_shared(q):
                    n = f * NPAIR + q
                    dve.wait_ge(shared_ready, n + 1)
                    xs = X[:, 2 * q:2 * q + 2, :].rearrange("p t d -> p (t d)")
                    dve.tensor_tensor(xs, xs, S[:, n % 2, :], ALU.add).then_inc(dve_added, 1)

                for i in range(SR):
                    weights_lo(i)
                for s in range(NP + 2):
                    if s - 1 in TAIL[3::4]:
                        add_shared(TAILQ + TAIL.index(s - 1) // 4)
                    if s < NP:
                        xd(s)
                    if s >= 2:
                        square(s - 2)
                    if SR <= s + 2 < NP:
                        weights_lo(s + 2)

            def combine(f, g):
                n = f * NC + g
                gs = slice(g * TC, (g + 1) * TC)
                dve.wait_ge(*shared_added(f, (g + 1) * TC // 2 - 1))
                for c in range(CHAINS):
                    m = n * CHAINS + c
                    paired = c == 1 and (f, g) in PAIRED
                    if paired:
                        dve.wait_ge(planes_paired, PAIRED.index((f, g)) + 1)
                    else:
                        dve.wait_ge(plane_loaded[m % PB], 16 * (m // PB + 1))
                    for h in range(1 if paired else 2):
                        link(dve.tensor_tensor(X[:, gs, :], X[:, gs, :], PL[:, m % PB, :, h, :], ALU.add))
                    dve.nop().then_inc(plane_used, 1)
                if f:
                    dve.nop().then_inc(x_final, 1)

            def attention(c):
                n = A_att + c * ATT_A
                dve.wait_ge(gT_ready, KD * (c + 1))
                if c:
                    dve.wait_ge(go_ready, c)
                for z, (dst, b) in enumerate(((ug, bu), (vg, bv))):
                    for r in range(KD):
                        u = n + 1 + KD + z * KD + r
                        dve.wait_ge(*full(A_full, u))
                        link(dve.scalar_tensor_tensor(out=dst[:, r, :], in0=psA[u % 2][:, :], scalar=b[:, r:r + 1],
                                                      in1=gT[:, r, :], op0=ALU.add, op1=ALU.mult))
                        dve.nop().then_inc(A_free[u % 2], 1)
                        dve.nop().then_inc(uv_used, 1)
                for r in range(KD):
                    for s in range(SEQ):
                        ins = dve.tensor_tensor_scan(cum[:, r, s * L:(s + 1) * L], ones, ug[:, r, s * L:(s + 1) * L],
                                                     0.0, ALU.mult, ALU.add)
                ins.then_inc(cum_ready, 1)

            def att_residual(c):
                for q in range(TC // 2):
                    u = C_att + c * TC // 2 + q
                    j = c * TC + 2 * q
                    dve.wait_ge(*full(C_full, u))
                    link(dve.tensor_tensor(X[:, j:j + 2, :], X[:, j:j + 2, :],
                                           psC[u % 2][:, :].rearrange("p (t d) -> p t d", d=D), ALU.add))
                    dve.nop().then_inc(C_free[u % 2], 1)

            for g in range(NC):
                dve.wait_ge(x_loaded[g], 16)
                stats(0, g)
                if g == 0:
                    constants()
                if g == 2:
                    dve.wait_ge(hi_made, 2)
                    link(dve.tensor_tensor(cb16[:, 1, :], cbs[:, :], cb16[:, 0, :], ALU.subtract))
                    link(dve.tensor_scalar(cb16[:, 1, :], cb16[:, 1, :], slotno[0:2, :], None, ALU.mult))
                    link(dve.scalar_tensor_tensor(out=cb16[:, 2, :], in0=cb16[:, 0, :], scalar=first_row, in1=cb16[:, 1, :],
                                                  op0=ALU.mult, op1=ALU.add))
                    dve.tensor_tensor(w16[:, 1, :], raw, w16[:, 0, :], ALU.subtract).then_inc(lo_made, 1)
            for g in range(NC):
                route(0, g)
            search(0, 0, NC)
            slots(0)
            experts(0)
            for g in range(NC - 1):
                combine(0, g)
                stats(1, g)
            for c in range(NC + 3):
                if c < NC:
                    attention(c)
                if c == 0:
                    combine(0, NC - 1)
                    stats(1, NC - 1)
                if c == NC - 1:
                    route(1, 0)
                    route(1, 1)
                if c == NC:
                    search(1, 0, 2)
                if c == NC + 1:
                    search(1, 2, 3)
                if 1 <= c <= NC:
                    att_residual(c - 1)
                    stats(2, c - 1)
                if NC <= c < NC + 2:
                    route(1, c - 2)
            search(1, 3, 4)
            slots(1)
            experts(1)
            for g in range(NC):
                combine(1, g)


def kernel(L0_attn_x, L0_attn_Wu, L0_attn_bu, L0_attn_Wv, L0_attn_bv, L0_attn_Wg1, L0_attn_bg1, L0_attn_Wg2,
           L0_attn_bg2, L0_attn_conv_w, L0_attn_conv_b, L0_ffn_gate_w, L0_ffn_e_bias, L0_ffn_w1, L0_ffn_w2,
           L0_ffn_shared_up_w, L0_ffn_shared_down_w):
    import numpy as np
    import concourse.bacc as bacc
    from concourse.bass_utils import run_bass_kernel_spmd

    def blocks(w):
        w = np.asarray(w)
        return np.ascontiguousarray(w.reshape(-1, P, w.shape[1]).transpose(1, 0, 2))

    x = np.asarray(L0_attn_x)
    B, L, D = x.shape
    T = B * L
    w1, w2 = np.asarray(L0_ffn_w1), np.asarray(L0_ffn_w2)
    E, I, _ = w1.shape
    KD = D // P
    w1l = w1.transpose(2, 0, 1).reshape(KD, P, E, I).transpose(1, 2, 0, 3).reshape(P, E, KD * I)
    w2l = w2.transpose(2, 0, 1)
    wexp = np.ascontiguousarray(np.concatenate([w1l, w2l], axis=2))
    col = lambda v: np.asarray(v).reshape(KD, P).T
    cw = np.asarray(L0_attn_conv_w)[:, 0, :]
    bg1 = np.asarray(L0_attn_bg1)
    vecs = np.ascontiguousarray(np.concatenate(
        [col(L0_attn_bu), col(L0_attn_bv), col(L0_attn_bg2),
         col(cw[:, 0]), col(cw[:, 1]), col(cw[:, 2]),
         np.pad(bg1, (0, P - bg1.size)).reshape(P, 1)], axis=1))
    p = np.arange(P)
    NP = E // 2
    sel = np.zeros((P, 2, 2, NP), np.float32)
    for e in range(E):
        sel[e, e % 2, 0, e // 2] = sel[E + e, e % 2, 1, e // 2] = 1
    turned = np.kron(np.eye(2), np.eye(P // 2)[::-1])
    g, c = np.divmod(np.arange(T // 2), 2 * P)
    keyrow = T - (g * 4 * P + p[:, None] // E * 2 * P + c)
    consts = np.ascontiguousarray(np.concatenate(
        [np.eye(P), np.ones((P, L)),
         np.stack([p < CAP, p >= CAP], 1), (p >= CAP)[:, None], p[:, None], sel.reshape(P, -1), turned],
        axis=1).astype(np.float32))
    arrays = {
        "x": np.ascontiguousarray(x.reshape(T, D)), "wexp": wexp,
        "ebias": np.ascontiguousarray(np.broadcast_to(np.asarray(L0_ffn_e_bias)[None, :], (P, E))),
        "wsplit": np.ascontiguousarray(np.concatenate(
            [blocks(np.asarray(w).T).reshape(P, -1) for w in
             (L0_ffn_gate_w, L0_ffn_shared_up_w, L0_attn_Wu, L0_attn_Wv, L0_attn_Wg1)], axis=1)),
        "sdown": blocks(np.asarray(L0_ffn_shared_down_w).T),
        "wu": blocks(np.asarray(L0_attn_Wu).T), "wg2": np.ascontiguousarray(np.asarray(L0_attn_Wg2).T),
        "convb": np.ascontiguousarray(np.broadcast_to(np.asarray(L0_attn_conv_b).reshape(1, D), (2, D))),
        "vecs": vecs, "consts": consts, "keys": np.ascontiguousarray(keyrow.astype(np.float32)),
    }
    nc = bacc.Bacc("TRN2", target_bir_lowering=False, num_devices=1)
    args = [nc.dram_tensor(n, a.shape, mybir.dt.from_np(a.dtype), kind="ExternalInput").ap() for n, a in arrays.items()]
    out = nc.dram_tensor("out", (T, D), F32, kind="ExternalOutput").ap()
    build(nc, *args, out)
    r = run_bass_kernel_spmd(nc, [arrays], core_ids=[0])
    return r.results[0]["out"].reshape(B, L, D)
```
